# Optimizing a Trainium2 kernel written in Bass

```python
import numpy as np
import jax
import jax.numpy as jnp

def _softmax(x, axis=-1):
    return jax.nn.softmax(x, axis=axis)

def _gelu(x):
    return jax.nn.gelu(x, approximate=True)

def _silu(x):
    return jax.nn.silu(x)

def _sigmoid(x):
    return jax.nn.sigmoid(x)

def _layernorm(x, axis=-1, eps=1e-05):
    m = jnp.mean(x, axis=axis, keepdims=True)
    v = jnp.var(x, axis=axis, keepdims=True)
    return (x - m) / jnp.sqrt(v + eps)

def _scatter_add(tgt, idx, src, axis=0):
    return tgt.at[idx].add(src)

def _segment_sum(src, seg, n):
    return jax.ops.segment_sum(src, seg, n)
kernel_name = 'mk_xattn_ffn_d1_seqx_r8_025cda'

def setup_inputs(seed: int=0):
    np.random.seed(seed)
    _w = jnp.asarray

    def _rec_inputs():
        import jax
        import jax.numpy as jnp
        _rk = jax.random.key(seed)
        x = 0.002226 + 0.9996 * jax.random.normal(jax.random.fold_in(_rk, 1), (128, 64, 128), jnp.float32)
        _lenS = 64 - jax.random.randint(jax.random.fold_in(_rk, 7), (128,), 0, max(1, 64 // 4) + 1, jnp.int32)
        _lenS2 = 64 - jax.random.randint(jax.random.fold_in(_rk, 8), (128,), 0, max(1, 64 // 4) + 1, jnp.int32)
        _ctx_1024P = jax.random.normal(jax.random.fold_in(_rk, 11), (128, 16, 128), jnp.float32)
        _ctx_1024c = jax.random.dirichlet(jax.random.fold_in(_rk, 511), 0.3 * jnp.ones((16,), jnp.float32), (128, 64))
        _ctx_1024t = jnp.einsum('bsk,bkd->bsd', _ctx_1024c, _ctx_1024P)
        _ctx_1024t = _ctx_1024t * jax.lax.rsqrt(jnp.mean(jnp.square(_ctx_1024t)) + 1e-12) * 0.953939
        ctx_1024 = -0.000125008 + 0.999885 * (_ctx_1024t + 0.3 * jax.random.normal(jax.random.fold_in(_rk, 611), (128, 64, 128), jnp.float32))
        _validS = jnp.arange(64)[None, :] < _lenS[:, None]
        _validS2 = jnp.arange(64)[None, :] < _lenS2[:, None]
        _causal = jnp.tril(jnp.ones((64, 64), dtype=bool))
        mask_BxS2_ik0 = jnp.where(jnp.broadcast_to(_validS2[:, :], (128, 64)), 0, 1).astype(jnp.int32)
        return (x, ctx_1024, mask_BxS2_ik0)
    x, ctx_1024, mask_BxS2_ik0 = _rec_inputs()

    def _L0_xattn_setup():
        import jax, jax.numpy as jnp
        import numpy as np
        LN_EPS = 1e-05

        def layer_norm(x, w, b):
            mu = jnp.mean(x, axis=-1, keepdims=True)
            var = jnp.mean(jnp.square(x - mu), axis=-1, keepdims=True)
            return (x - mu) * jax.lax.rsqrt(var + LN_EPS) * w + b
        key = jax.random.key(seed)
        ks = jax.random.split(key, 8)
        B, F, Q, D = (8, 512, 64, 128)
        H, DH = (16, 64)
        inner = H * DH
        s = 1.0 / np.sqrt(D)
        return {'features': jax.random.normal(ks[0], (B, F, D), jnp.float32), 'latents': jax.random.normal(ks[1], (B, Q, D), jnp.float32), 'key_attention_mask': jax.random.randint(ks[2], (B, F), 0, 2, jnp.int32), 'ln_m_w': jnp.ones((D,), jnp.float32), 'ln_m_b': jnp.zeros((D,), jnp.float32), 'ln_l_w': jnp.ones((D,), jnp.float32), 'ln_l_b': jnp.zeros((D,), jnp.float32), 'Wq': jax.random.normal(ks[3], (D, inner), jnp.float32) * s, 'Wk': jax.random.normal(ks[4], (D, inner), jnp.float32) * s, 'Wv': jax.random.normal(ks[5], (D, inner), jnp.float32) * s, 'Wo': jax.random.normal(ks[6], (inner, D), jnp.float32) * (1.0 / np.sqrt(inner))}
    _L0_xattn_all = _L0_xattn_setup()
    _L0_xattn_in = {k: v for k, v in _L0_xattn_all.items() if k in ('ln_m_w', 'ln_m_b', 'ln_l_w', 'ln_l_b', 'Wq', 'Wk', 'Wv', 'Wo')}
    del _L0_xattn_all

    def _L0_ffn_setup():
        import jax, jax.numpy as jnp
        import numpy as np
        B, S, D = (1, 256, 128)
        E, K, H = (8, 2, 64)
        HS = 128
        key = jax.random.key(seed)
        ks = jax.random.split(key, 8)
        sc = lambda fan_in: 1.0 / np.sqrt(fan_in)
        return {'x': jax.random.normal(ks[0], (B, S, D), jnp.float32), 'gate_w': jax.random.normal(ks[1], (D, E), jnp.float32) * sc(D), 'w1': jax.random.normal(ks[2], (E, D, H), jnp.float32) * sc(D), 'w3': jax.random.normal(ks[3], (E, D, H), jnp.float32) * sc(D), 'w2': jax.random.normal(ks[4], (E, H, D), jnp.float32) * sc(H), 'ws1': jax.random.normal(ks[5], (D, HS), jnp.float32) * sc(D), 'ws3': jax.random.normal(ks[6], (D, HS), jnp.float32) * sc(D), 'ws2': jax.random.normal(ks[7], (HS, D), jnp.float32) * sc(HS)}
    _L0_ffn_all = _L0_ffn_setup()
    _L0_ffn_in = {k: v for k, v in _L0_ffn_all.items() if k in ('gate_w', 'w1', 'w3', 'w2', 'ws1', 'ws3', 'ws2')}
    del _L0_ffn_all
    return {'x': x, 'ctx_1024': ctx_1024, 'mask_BxS2_ik0': mask_BxS2_ik0, 'L0_xattn_ln_m_w': _L0_xattn_in['ln_m_w'], 'L0_xattn_ln_m_b': _L0_xattn_in['ln_m_b'], 'L0_xattn_ln_l_w': _L0_xattn_in['ln_l_w'], 'L0_xattn_ln_l_b': _L0_xattn_in['ln_l_b'], 'L0_xattn_Wq': _L0_xattn_in['Wq'], 'L0_xattn_Wk': _L0_xattn_in['Wk'], 'L0_xattn_Wv': _L0_xattn_in['Wv'], 'L0_xattn_Wo': _L0_xattn_in['Wo'], 'L0_ffn_gate_w': _L0_ffn_in['gate_w'], 'L0_ffn_w1': _L0_ffn_in['w1'], 'L0_ffn_w3': _L0_ffn_in['w3'], 'L0_ffn_w2': _L0_ffn_in['w2'], 'L0_ffn_ws1': _L0_ffn_in['ws1'], 'L0_ffn_ws3': _L0_ffn_in['ws3'], 'L0_ffn_ws2': _L0_ffn_in['ws2']}

def reference(x, ctx_1024, mask_BxS2_ik0, L0_xattn_ln_m_w, L0_xattn_ln_m_b, L0_xattn_ln_l_w, L0_xattn_ln_l_b, L0_xattn_Wq, L0_xattn_Wk, L0_xattn_Wv, L0_xattn_Wo, L0_ffn_gate_w, L0_ffn_w1, L0_ffn_w3, L0_ffn_w2, L0_ffn_ws1, L0_ffn_ws3, L0_ffn_ws2):
    import jax
    import jax.numpy as jnp

    def _L0_xattn_ref(features, latents, key_attention_mask, ln_m_w, ln_m_b, ln_l_w, ln_l_b, Wq, Wk, Wv, Wo):
        import jax, jax.numpy as jnp
        import numpy as np
        LN_EPS = 1e-05

        def layer_norm(x, w, b):
            mu = jnp.mean(x, axis=-1, keepdims=True)
            var = jnp.mean(jnp.square(x - mu), axis=-1, keepdims=True)
            return (x - mu) * jax.lax.rsqrt(var + LN_EPS) * w + b
        H, DH = (16, 64)
        B, F, D = features.shape
        Q = latents.shape[1]
        scale = DH ** (-0.5)
        x = layer_norm(features, ln_m_w, ln_m_b)
        lat = layer_norm(latents, ln_l_w, ln_l_b)
        q = (lat @ Wq).reshape(B, Q, H, DH).transpose(0, 2, 1, 3)
        kv_in = jnp.concatenate([x, lat], axis=1)
        k = (kv_in @ Wk).reshape(B, F + Q, H, DH).transpose(0, 2, 1, 3)
        v = (kv_in @ Wv).reshape(B, F + Q, H, DH).transpose(0, 2, 1, 3)
        q = q * scale
        sim = jnp.einsum('bhqd,bhfd->bhqf', q, k)
        full_mask = jnp.concatenate([key_attention_mask, jnp.ones((B, Q), key_attention_mask.dtype)], axis=1)
        sim = jnp.where(full_mask[:, None, None, :] == 0, -jnp.inf, sim)
        sim = sim - jax.lax.stop_gradient(jnp.max(sim, axis=-1, keepdims=True))
        alphas = jax.nn.softmax(sim, axis=-1)
        out = jnp.einsum('bhqf,bhfv->bhqv', alphas, v)
        out = out.transpose(0, 2, 1, 3).reshape(B, Q, H * DH)
        return out @ Wo

    def _L0_ffn_ref(x, gate_w, w1, w3, w2, ws1, ws3, ws2):
        import jax, jax.numpy as jnp
        import numpy as np
        B, S, D = (1, 256, 128)
        E, K, H = (8, 2, 64)
        HS = 128
        b, s, d = x.shape
        xt = x.reshape(-1, d)
        T = xt.shape[0]
        scores = jax.nn.sigmoid(xt @ gate_w)
        top_scores, top_idx = jax.lax.top_k(scores, K)
        top_scores = top_scores / jnp.sum(top_scores, axis=-1, keepdims=True)
        dense = jnp.zeros((T, E), xt.dtype).at[jnp.arange(T)[:, None], top_idx].set(top_scores)
        h = jax.nn.silu(jnp.einsum('td,edh->teh', xt, w1)) * jnp.einsum('td,edh->teh', xt, w3)
        y = jnp.einsum('teh,ehd->ted', h, w2)
        routed = jnp.einsum('ted,te->td', y, dense)
        shared = jax.nn.silu(xt @ ws1) * (xt @ ws3) @ ws2
        return (shared + routed).reshape(b, s, d)
    x = x + _L0_xattn_ref(ctx_1024, _layernorm(x, axis=-1), mask_BxS2_ik0, L0_xattn_ln_m_w, L0_xattn_ln_m_b, L0_xattn_ln_l_w, L0_xattn_ln_l_b, L0_xattn_Wq, L0_xattn_Wk, L0_xattn_Wv, L0_xattn_Wo)
    x = x + _L0_ffn_ref(_layernorm(x, axis=-1), L0_ffn_gate_w, L0_ffn_w1, L0_ffn_w3, L0_ffn_w2, L0_ffn_ws1, L0_ffn_ws3, L0_ffn_ws2)
    return x

_drawn_inputs = setup_inputs


def setup_inputs(seed=0):
    import zlib

    import numpy as np

    out = dict(_drawn_inputs(seed))
    spreads = {'L0_xattn_ln_m_w': (1.0, 0.2),
     'L0_xattn_ln_m_b': (0.0, 0.1),
     'L0_xattn_ln_l_w': (1.0, 0.2),
     'L0_xattn_ln_l_b': (0.0, 0.1)}
    factors = {}
    for name, (base, spread) in spreads.items():
        noise = np.random.default_rng([zlib.crc32(name.encode()), seed]).standard_normal(out[name].shape)
        drawn = base * np.exp(spread * noise) if base else spread * noise
        out[name] = jnp.asarray(drawn.astype(out[name].dtype))
    for name, factor in factors.items():
        out[name] = (out[name] * factor).astype(out[name].dtype)
    return out
```

```python
import concourse.bass as bass
from concourse import mybir
from contextlib import ExitStack


def xattn_moe_ffn_kernel(nc, x, ctx, mask, ln_m_w, ln_m_b, ln_l_w, ln_l_b, Wq, Wk, Wv, Wo,
                         gate_w, w1, w3, w2, ws1, ws3, ws2, out):
    fp32 = mybir.dt.float32
    f32r = mybir.dt.float32r
    ALU = mybir.AluOpType
    ACT = mybir.ActivationFunctionType
    AX = mybir.AxisListType

    P = 128
    B, S, D = x.shape
    INNER = Wq.shape[1]
    DH = 64
    H = INNER // DH
    E, _, FH = w1.shape
    EPS = 1e-5
    SCALE = float(DH) ** -0.5
    BIG = 1e30
    GB = 4
    NG = B // GB
    GT = GB * S
    HALVES = 2 * GB
    PAIRS = 4
    NT = E * FH // P
    TT = GT // P

    es = ExitStack()
    with es:
        def sb(name, shape, dt=fp32):
            return es.enter_context(nc.sbuf_tensor(name, shape, dt))

        def sem(name):
            return es.enter_context(nc.semaphore(name))

        MV_hi = [sb(f"MV_hi{n}", [P, H, D], f32r) for n in range(2)]
        MV_lo = [sb(f"MV_lo{n}", [P, H, D], f32r) for n in range(2)]
        w13_hi = sb("w13_hi", [P, 2, NT + 1, P], f32r)
        w13_lo = sb("w13_lo", [P, 2, NT + 1, P], f32r)
        w2_sb = sb("w2_sb", [P, NT + 1, D])
        gate_sb = sb("gate_sb", [P, E])
        ln_w_bc = sb("ln_w_bc", [P, D])
        ln_b_bc = sb("ln_b_bc", [P, D])
        ident = sb("ident", [P, P])
        expert_rows = sb("expert_rows", [2 * E, NT, 2, FH])
        expert_rows_r = sb("expert_rows_r", [2 * E, NT, 2, FH], f32r)
        before = sb("before", [P, E, E])
        var_mul = sb("var_mul", [P, 1])
        var_add = sb("var_add", [P, 1])
        minus_half = sb("minus_half", [P, GB])
        eps_col = sb("eps_col", [P, 1])

        kv_raw = [sb(f"kv_raw{n}", [P, GB, D]) for n in range(2)]
        kv_bn = sb("kv_bn", [P, GB, 6])
        kv_mv = sb("kv_mv", [P, GB, 2])
        kv_ve = sb("kv_ve", [P, GB])
        kv_r = sb("kv_r", [P, GB])
        kv_n = sb("kv_n", [P, GB, D])
        kv_nw = sb("kv_nw", [P, GB, D])
        kv_f = sb("kv_f", [P, GB, D])
        kv_hi = [sb(f"kv_hi{n}", [P, GB, D], f32r) for n in range(2)]
        kv_lo = [sb(f"kv_lo{n}", [P, GB, D], f32r) for n in range(2)]
        kvT = [sb(f"kvT{n}", [P, GB, P]) for n in range(2)]
        latT_hi = [sb(f"latT_hi{n}", [P, GB, S], f32r) for n in range(2)]
        latT_lo = [sb(f"latT_lo{n}", [P, GB, S], f32r) for n in range(2)]
        tT = sb("tT", [P, GB, H, S])
        mask_raw = [sb(f"mask_raw{n}", [P, GB, S], mybir.dt.int32) for n in range(2)]
        mask_add = [sb(f"mask_add{n}", [P, GB, P]) for n in range(2)]
        logits = [sb(f"logits{n}", [P, PAIRS, P]) for n in range(2)]
        neg_max = [sb(f"neg_max{n}", [P, PAIRS]) for n in range(2)]
        probs = [sb(f"probs{n}", [P, PAIRS, P]) for n in range(2)]
        denom = [sb(f"denom{n}", [P, PAIRS]) for n in range(2)]
        rdenom = [sb(f"rdenom{n}", [P, PAIRS]) for n in range(2)]
        pT_hi = [sb(f"pT_hi{n}", [P, PAIRS * P], f32r) for n in range(2)]
        pT_lo = [sb(f"pT_lo{n}", [P, PAIRS * P], f32r) for n in range(2)]
        attnT = sb("attnT", [P, GT])
        x_res = [sb(f"x_res{n}", [P, TT, D]) for n in range(2)]
        x1 = [sb(f"x1_{n}", [P, TT, D]) for n in range(2)]
        x1_bn = sb("x1_bn", [P, TT, 6])
        x1_mv = sb("x1_mv", [P, TT, 2])
        x1_ve = sb("x1_ve", [P, TT])
        x1_r = sb("x1_r", [P, TT])
        x2 = sb("x2", [P, TT, D])
        x2T = sb("x2T", [P, GT])
        x2T_hi = sb("x2T_hi", [P, GT], f32r)
        x2T_lo = sb("x2T_lo", [P, GT], f32r)
        g_exp = sb("g_exp", [P, TT, E])
        g_one = sb("g_one", [P, TT, E])
        g_score = sb("g_score", [P, TT, E])
        g_gt = sb("g_gt", [P, TT, E, E])
        g_eq = sb("g_eq", [P, TT, E, E])
        g_tie = sb("g_tie", [P, TT, E, E])
        g_ahead = sb("g_ahead", [P, TT, E, E])
        g_rank = sb("g_rank", [P, TT, E])
        g_keep = sb("g_keep", [P, TT, E])
        g_sum = sb("g_sum", [P, TT])
        g_rsum = sb("g_rsum", [P, TT])
        g_dense = sb("g_dense", [P, TT, E])
        g_parts = sb("g_parts", [P, TT, 2, E])
        denseT = sb("denseT", [2 * E, GT], f32r)
        h_tanh = sb("h_tanh", [P, GT])
        h_silu = sb("h_silu", [P, GT])
        h_prod = sb("h_prod", [P, GT])
        h = sb("h", [P, NT + 1, GT])
        out_sb = [sb(f"out_sb{n}", [P, TT, D]) for n in range(2)]

        with ExitStack() as setup_only:
            def su(name, shape):
                return setup_only.enter_context(nc.sbuf_tensor(name, shape, fp32))

            wq_raw = su("wq_raw", [P, INNER])
            wk_raw = su("wk_raw", [P, INNER])
            wv_raw = su("wv_raw", [P, INNER])
            wo_raw = su("wo_raw", [P, H // 2, D])
            wT = [su(f"wT{n}", [P, H // 2, D]) for n in range(3)]
            w13_stage = [su(f"w13_stage{n}", [P, (NT + 1) * P]) for n in range(2)]
            MV_stage = [su(f"MV_stage{n}", [P, H, D]) for n in range(2)]
        cT_hi = [sb(f"cT_hi{n}", [P, H, GB, S], f32r) for n in range(2)]
        cT_lo = [sb(f"cT_lo{n}", [P, H, GB, S], f32r) for n in range(2)]

        banks = [es.enter_context(nc.psum_tensor(f"bank{n}", [P, 512], fp32)) for n in range(8)]
        S_ps, PT_ps, C_ps, T_ps, W_ps, H_ps, X_ps, Y_ps = banks

        kv_loaded = [sem(f"kv_loaded{n}") for n in range(2)]
        mask_loaded = [sem(f"mask_loaded{n}") for n in range(2)]
        x_res_loaded = [sem(f"x_res_loaded{n}") for n in range(2)]
        attn_w_loaded = sem("attn_w_loaded")
        ffn_w_loaded = sem("ffn_w_loaded")
        ln_w_loaded = sem("ln_w_loaded")
        out_stored = [sem(f"out_stored{n}") for n in range(2)]
        waits_held = sem("waits_held")
        const_set = sem("const_set")
        consts_ready = sem("consts_ready")
        dve_consts = sem("dve_consts")
        wT_in_psum = sem("wT_in_psum")
        wT_ready = sem("wT_ready")
        MV_in_psum = sem("MV_in_psum")
        M_evac = sem("M_evac")
        V_evac = sem("V_evac")
        w_hi_done = sem("w_hi_done")
        w_split = sem("w_split")
        kv_bn_done = sem("kv_bn_done")
        kv_mv_done = sem("kv_mv_done")
        kv_step = sem("kv_step")
        kvT_in_psum = sem("kvT_in_psum")
        kvT_ready = sem("kvT_ready")
        latT_hi_ready = sem("latT_hi_ready")
        latT_lo_ready = sem("latT_lo_ready")
        t_in_psum = sem("t_in_psum")
        t_ready = sem("t_ready")
        mask_ready = sem("mask_ready")
        S_in_psum = sem("S_in_psum")
        logits_ready = sem("logits_ready")
        exp_done = sem("exp_done")
        rdenom_ready = sem("rdenom_ready")
        probs_ready = sem("probs_ready")
        pT_in_psum = sem("pT_in_psum")
        pT_hi_ready = sem("pT_hi_ready")
        pT_lo_ready = sem("pT_lo_ready")
        C_in_psum = sem("C_in_psum")
        cT_hi_ready = sem("cT_hi_ready")
        cT_lo_ready = sem("cT_lo_ready")
        W_in_psum = sem("W_in_psum")
        attnT_ready = sem("attnT_ready")
        attn_in_psum = sem("attn_in_psum")
        x1_step = sem("x1_step")
        x2_step = sem("x2_step")
        x2T_in_psum = sem("x2T_in_psum")
        x2T_ready = sem("x2T_ready")
        x2T_hi_ready = sem("x2T_hi_ready")
        x2T_lo_ready = sem("x2T_lo_ready")
        gate_in_psum = sem("gate_in_psum")
        gate_exp_done = sem("gate_exp_done")
        gate_step = sem("gate_step")
        denseT_in_psum = sem("denseT_in_psum")
        denseT_ready = sem("denseT_ready")
        H_in_psum = sem("H_in_psum")
        tanh_done = sem("tanh_done")
        silu_done = sem("silu_done")
        h_prod_done = sem("h_prod_done")
        h_routed_done = sem("h_routed_done")
        y_in_psum = sem("y_in_psum")
        out_ready = sem("out_ready")

        GATE_STEPS = 13
        KV_STEPS = 7
        HT = NT + 1

        block = es.enter_context(nc.Block())

        def after(eng, semaphore, count):
            if not isinstance(count, int) or count > 0:
                eng.wait_ge(semaphore, count)

        def frames(eng, frame):
            for i in (-1, 0, 1):
                frame(i // 2, i % 2)
            with eng.Fori(1, NG // 2 - 1) as j:
                frame(j, 0)
                frame(j, 1)
            for i in (NG - 2, NG - 1, NG, NG + 1):
                frame(i // 2, i % 2)

        def has(j, c, first, last):
            return not isinstance(j, int) or first <= 2 * j + c <= last

        def bank_heads(q):
            return slice(8 * (q // 2) + q % 2, 8 * (q // 2) + 8, 2)

        def hold_waits(eng):
            eng.sem_inc(waits_held, 1)

        def ffn_tile(j, p, k):
            i = 2 * j + p
            if k == 7 and has(j, p, 1, NG):
                return NT, HT * (i - 1)
            if k in (0, 1, 4, 5) and has(j, p, 2, NG + 1):
                r = (0, 1, 4, 5).index(k)
                return r, HT * (i - 2) + 1 + r
            return None

        @block.sync
        def _(sp):
            def load_kv(j, c):
                g, par = 2 * j + c, c % 2
                half = j + c // 2
                after(sp, kv_step, KV_STEPS * (g - 2) + 3)
                sp.dma_start(kv_raw[par][0:S, :, :], ctx[bass.ds(GB * g, GB), :, :].rearrange("b s d -> s b d")
                             ).then_inc(kv_loaded[par], 16)
                sp.dma_start(kv_raw[par][S:P, :, :], x[bass.ds(GB * g, GB), :, :].rearrange("b s d -> s b d")
                             ).then_inc(kv_loaded[par], 16)
                after(sp, mask_ready, g - 1)
                sp.dma_start(mask_raw[par][:, :, :], mask[bass.ds(GB * g, GB), :].partition_broadcast(P)
                             ).then_inc(mask_loaded[par], 16)

            load_kv(0, 0)
            for dst, src in ((wq_raw, Wq), (wk_raw, Wk), (wv_raw, Wv)):
                sp.dma_start(dst[:, :], src).then_inc(attn_w_loaded, 16)
            sp.dma_start(wo_raw[:, :, :], Wo.rearrange("(c p) n -> p c n", p=P)).then_inc(attn_w_loaded, 16)
            for dst, m, l in ((ln_w_bc, ln_m_w, ln_l_w), (ln_b_bc, ln_m_b, ln_l_b)):
                sp.dma_start(dst[0:S, :], m.partition_broadcast(S)).then_inc(ln_w_loaded, 16)
                sp.dma_start(dst[S:P, :], l.partition_broadcast(S)).then_inc(ln_w_loaded, 16)
            for n, (w, ws) in enumerate(((w1, ws1), (w3, ws3))):
                stage = w13_stage[n]
                sp.dma_start(stage[:, 0:NT * P].rearrange("p (e f) -> p e f", e=E),
                             w.rearrange("e d f -> d e f")).then_inc(ffn_w_loaded, 16)
                sp.dma_start(stage[:, NT * P:HT * P], ws).then_inc(ffn_w_loaded, 16)
            sp.dma_start(w2_sb[:, 0:NT, :], w2.rearrange("(i e) f d -> (e f) i d", e=2)).then_inc(ffn_w_loaded, 16)
            sp.dma_start(w2_sb[:, NT, :], ws2).then_inc(ffn_w_loaded, 16)
            sp.dma_start(gate_sb[:, :], gate_w).then_inc(ffn_w_loaded, 16)

            def frame(j, p):
                i = 2 * j + p
                if has(j, p, -1, NG - 3):
                    load_kv(j, p + 2)
                if has(j, p, 0, NG - 1):
                    after(sp, x1_step, 3 * (i - 2) + 1)
                    sp.dma_start(x_res[p][:, :, :],
                                 x.rearrange("b s d -> (b s) d")[bass.ds(GT * i, GT), :].rearrange("(t q) d -> q t d", q=P)
                                 ).then_inc(x_res_loaded[p], 16)
                if has(j, p, 2, NG + 1):
                    after(sp, out_ready, TT * (i - 1))
                    sp.dma_start(out.rearrange("b s d -> (b s) d")[bass.ds(GT * (i - 2), GT), :].rearrange("(t q) d -> q t d", q=P),
                                 out_sb[p][:, :, :]).then_inc(out_stored[p], 16)

            frames(sp, frame)
            for n in range(2):
                sp.wait_ge(out_stored[n], 16 * (NG // 2))

        @block.gpsimd
        def _(pool):
            for n, (ap, value) in enumerate((
                    (ident[:, :], 0.0), (expert_rows[:, :, :, :], 0.0), (before[:, :, :], 1.0),
                    (var_mul[0:S, :], 1.0), (var_mul[S:P, :], 1.0 + EPS),
                    (var_add[0:S, :], EPS), (var_add[S:P, :], EPS * EPS),
                    (minus_half[:, :], -0.5), (eps_col[:, :], EPS),
                    (mask_add[0][:, :, :], 0.0), (mask_add[1][:, :, :], 0.0))):
                nc.gpsimd.memset(ap, value).then_inc(const_set, 1)
                pool.wait_ge(const_set, n + 1)
            nc.gpsimd.affine_select(out=ident[:, :], in_=ident[:, :], compare_op=ALU.not_equal, fill=1.0,
                                    base=0, pattern=[[-1, P]], channel_multiplier=1).then_inc(consts_ready, 1)
            nc.gpsimd.affine_select(out=expert_rows[:, :, :, :], in_=expert_rows[:, :, :, :],
                                    compare_op=ALU.not_equal, fill=1.0, base=0,
                                    pattern=[[-2, NT], [-1, 2], [0, FH]], channel_multiplier=1).then_inc(const_set, 1)
            pool.wait_ge(const_set, 12)
            nc.gpsimd.affine_select(out=expert_rows[:, :, :, :], in_=expert_rows[:, :, :, :],
                                    compare_op=ALU.not_equal, fill=1.0, base=-E,
                                    pattern=[[-2, NT], [-1, 2], [0, FH]], channel_multiplier=1).then_inc(const_set, 1)
            nc.gpsimd.affine_select(out=before[:, :, :], in_=before[:, :, :], compare_op=ALU.is_gt, fill=0.0,
                                    base=0, pattern=[[1, E], [-1, E]], channel_multiplier=0).then_inc(const_set, 1)
            pool.wait_ge(const_set, 14)
            nc.gpsimd.tensor_copy(expert_rows_r[:, :, :, :], expert_rows[:, :, :, :]).then_inc(consts_ready, 1)

            def kv_stats_to_keys(j, c):
                g, par = 2 * j + c, c % 2
                step = KV_STEPS * g
                pool.wait_ge(kv_mv_done, g + 1)
                hold_waits(pool)
                nc.gpsimd.tensor_scalar(kv_ve[:, :], kv_mv[:, :, 1], var_mul[:, 0:1], var_add[:, 0:1],
                                        ALU.mult, ALU.add).then_inc(kv_step, 1)
                pool.wait_ge(kv_step, step + 1)
                nc.gpsimd.tensor_tensor(kv_r[:, :], kv_ve[:, :], minus_half[:, :], ALU.pow).then_inc(kv_step, 1)
                pool.wait_ge(kv_step, step + 2)
                hold_waits(pool)
                for b in range(GB):
                    last = nc.gpsimd.tensor_scalar(kv_n[:, b, :], kv_raw[par][:, b, :], kv_mv[:, b, 0:1],
                                                   kv_r[:, b:b + 1], ALU.subtract, ALU.mult)
                last.then_inc(kv_step, 1)
                pool.wait_ge(kv_step, step + 3)
                if isinstance(j, int) and g == 0:
                    pool.wait_ge(ln_w_loaded, 64)
                nc.gpsimd.tensor_tensor(kv_nw[:, :, :], kv_n[:, :, :],
                                        ln_w_bc[:, :].unsqueeze(1).broadcast_to([P, GB, D]), ALU.mult).then_inc(kv_step, 1)
                pool.wait_ge(kv_step, step + 4)
                after(pool, kvT_in_psum, g)
                nc.gpsimd.tensor_tensor(kv_f[:, :, :], kv_nw[:, :, :],
                                        ln_b_bc[:, :].unsqueeze(1).broadcast_to([P, GB, D]), ALU.add).then_inc(kv_step, 1)

            def split_keys(j, c):
                g, par = 2 * j + c, c % 2
                step = KV_STEPS * g
                after(pool, C_in_psum, HALVES * (g - 1))
                pool.wait_ge(kv_step, step + 5)
                hold_waits(pool)
                nc.gpsimd.tensor_copy(kv_hi[par][:, :, :], kv_f[:, :, :]).then_inc(kv_step, 1)
                pool.wait_ge(kv_step, step + 6)
                nc.gpsimd.tensor_tensor(kv_lo[par][:, :, :], kv_f[:, :, :], kv_hi[par][:, :, :].bitcast(fp32),
                                        ALU.subtract).then_inc(kv_step, 1)

            def split_weights(n, evac):
                for q in range(4):
                    pool.wait_ge(evac, q + 1)
                    heads = bank_heads(q)
                    nc.gpsimd.tensor_copy(MV_hi[n][:, heads, :], MV_stage[n][:, heads, :]).then_inc(w_hi_done, 1)
                    pool.wait_ge(w_hi_done, 4 * n + q + 1)
                    nc.gpsimd.tensor_tensor(MV_lo[n][:, heads, :], MV_stage[n][:, heads, :],
                                            MV_hi[n][:, heads, :].bitcast(fp32), ALU.subtract).then_inc(w_split, 1)

            def frame(j, p):
                i = 2 * j + p
                for k in range(HALVES):
                    e = HALVES * i + k
                    if has(j, p, 0, NG - 1):
                        pool.wait_ge(rdenom_ready, e + 1)
                        nc.gpsimd.tensor_tensor(probs[k % 2][:, :, :], probs[k % 2][:, :, :],
                                                rdenom[k % 2][:, :].unsqueeze(2).broadcast_to([P, PAIRS, P]),
                                                ALU.mult).then_inc(probs_ready, 1)
                    if k == 0 and has(j, p, -1, NG - 2):
                        kv_stats_to_keys(j, p + 1)
                    if k == 1 and has(j, p, -1, NG - 2):
                        split_keys(j, p + 1)
                        if isinstance(j, int) and i == -1:
                            split_weights(0, M_evac)
                            split_weights(1, V_evac)
                    if k == 5 and has(j, p, 1, NG):
                        step = 3 * (i - 1)
                        pool.wait_ge(x1_step, step + 3)
                        hold_waits(pool)
                        nc.gpsimd.tensor_scalar(x1_ve[:, :], x1_mv[:, :, 1], 1.0, eps_col[:, 0:1],
                                                ALU.mult, ALU.add).then_inc(x2_step, 1)
                        pool.wait_ge(x2_step, step + 1)
                        nc.gpsimd.tensor_tensor(x1_r[:, :], x1_ve[:, :], minus_half[:, 0:TT],
                                                ALU.pow).then_inc(x2_step, 1)
                        pool.wait_ge(x2_step, step + 2)
                        after(pool, x2T_in_psum, i - 1)
                        hold_waits(pool)
                        for t in range(TT):
                            last = nc.gpsimd.tensor_scalar(x2[:, t, :], x1[(p + 1) % 2][:, t, :], x1_mv[:, t, 0:1],
                                                           x1_r[:, t:t + 1], ALU.subtract, ALU.mult)
                        last.then_inc(x2_step, 1)

            frames(pool, frame)

        @block.scalar
        def _(act):
            for q in range(4):
                act.wait_ge(MV_in_psum, q + 1)
                nc.scalar.mul(MV_stage[0][:, bank_heads(q), :], banks[q][:, :].rearrange("p (h d) -> p h d", h=4),
                              -SCALE).then_inc(M_evac, 1)
            for q in range(4):
                act.wait_ge(MV_in_psum, 4 + q + 1)
                nc.scalar.copy(MV_stage[1][:, bank_heads(q), :],
                               banks[4 + q][:, :].rearrange("p (h d) -> p h d", h=4)).then_inc(V_evac, 1)

            def frame(j, p):
                i = 2 * j + p
                for k in range(HALVES):
                    e = HALVES * i + k
                    prev = has(j, p, 0, NG - 1) if k else has(j, p, 1, NG)
                    kp = (k - 1) % HALVES
                    par = p if k else (p + 1) % 2
                    if prev:
                        act.wait_ge(pT_in_psum, e)
                        after(act, C_in_psum, e - 2)
                        nc.scalar.copy(pT_hi[kp % 2][:, :], PT_ps[:, :]).then_inc(pT_hi_ready, 1)
                    if has(j, p, 0, NG - 1):
                        for r in range(PAIRS):
                            act.wait_ge(logits_ready, PAIRS * e + r + 1)
                            if r == 0:
                                after(act, pT_in_psum, e - 1)
                            nc.scalar.activation(probs[k % 2][:, r, :], logits[k % 2][:, r, :], ACT.Exp,
                                                 bias=neg_max[k % 2][:, r:r + 1], scale=-1.0,
                                                 accum_out=denom[k % 2][:, r:r + 1]).then_inc(exp_done, 1)
                    if k == 3 and has(j, p, -1, NG - 2):
                        par1 = (p + 1) % 2
                        act.wait_ge(kvT_in_psum, i + 2)
                        after(act, S_in_psum, HALVES * i)
                        nc.scalar.copy(kvT[par1][:, :, :], X_ps[:, :].rearrange("p (b f) -> p b f", b=GB)
                                       ).then_inc(kvT_ready, 1)
                        after(act, t_in_psum, HALVES * i)
                        nc.scalar.copy(latT_hi[par1][:, :, :],
                                       X_ps[:, :].rearrange("p (b f) -> p b f", b=GB)[:, :, S:P]
                                       ).then_inc(latT_hi_ready, 1)
                    if (has(j, p, 0, NG - 1) if k < 4 else has(j, p, -1, NG - 2)):
                        c = (k + 4) % HALVES
                        n = e + 4
                        act.wait_ge(t_in_psum, n + 1)
                        after(act, S_in_psum, (HALVES * (i - 1) + 8) if k < 4 else (HALVES * i + 4))
                        nc.scalar.copy(tT[:, :, 2 * c:2 * c + 2, :].rearrange("p b h q -> p h b q"),
                                       T_ps[:, :].rearrange("p (h b q) -> p h b q", h=2, b=GB)).then_inc(t_ready, 1)
                    if prev:
                        act.wait_ge(C_in_psum, e)
                        if kp == 0:
                            after(act, W_in_psum, i - 1)
                        nc.scalar.copy(cT_hi[par][:, 8 * (kp // 4):8 * (kp // 4) + 8, kp % 4, :],
                                       C_ps[:, :].rearrange("p (h q) -> p h q", h=8)).then_inc(cT_hi_ready, 1)
                    if k == 4 and has(j, p, 1, NG):
                        act.wait_ge(W_in_psum, i)
                        after(act, attn_in_psum, i - 1)
                        nc.scalar.copy(attnT[:, :], W_ps[:, 0:GT]).then_inc(attnT_ready, 1)
                    if k == 6 and has(j, p, 1, NG):
                        act.wait_ge(x2T_in_psum, i)
                        after(act, gate_in_psum, i - 1)
                        nc.scalar.copy(x2T[:, :], X_ps[:, 0:GT]).then_inc(x2T_ready, 1)
                        after(act, H_in_psum, HT * (i - 1))
                        nc.scalar.copy(x2T_hi[:, :], X_ps[:, 0:GT]).then_inc(x2T_hi_ready, 1)
                    if k == 7 and has(j, p, 1, NG):
                        act.wait_ge(gate_in_psum, i)
                        after(act, gate_step, GATE_STEPS * (i - 2) + 1)
                        nc.scalar.activation(g_exp[:, :, :], X_ps[:, 0:TT * E].rearrange("p (t e) -> p t e", e=E),
                                             ACT.Exp, scale=-1.0).then_inc(gate_exp_done, 1)
                    tile = ffn_tile(j, p, k)
                    if tile is not None:
                        n = tile[1]
                        act.wait_ge(H_in_psum, n + 1)
                        after(act, silu_done, n)
                        nc.scalar.activation(h_tanh[:, :], H_ps[:, 0:GT], ACT.Tanh, scale=0.5).then_inc(tanh_done, 1)

            frames(act, frame)

        @block.vector
        def _(dve):
            for n in range(6):
                dve.wait_ge(wT_in_psum, n + 1)
                nc.vector.tensor_copy(wT[n // 2][:, 4 * (n % 2):4 * (n % 2) + 4, :],
                                      banks[n][:, :].rearrange("p (c d) -> p c d", c=4)).then_inc(wT_ready, 1)
            dve.wait_ge(ffn_w_loaded, 7 * 16)
            for n in range(2):
                nc.vector.tensor_copy(w13_hi[:, n, :, :],
                                      w13_stage[n][:, :].rearrange("p (t f) -> p t f", f=P)).then_inc(dve_consts, 1)
            nc.vector.tensor_scalar(w2_sb[:, :, :], w2_sb[:, :, :], 0.5, None, ALU.mult).then_inc(dve_consts, 1)
            dve.wait_ge(dve_consts, 3)
            for n in range(2):
                nc.vector.tensor_tensor(w13_lo[:, n, :, :], w13_stage[n][:, :].rearrange("p (t f) -> p t f", f=P),
                                        w13_hi[:, n, :, :].bitcast(fp32), ALU.subtract).then_inc(dve_consts, 1)
            dve.wait_ge(const_set, 14)
            dve.wait_ge(dve_consts, 5)

            def convert_mask(j, c):
                g, par = 2 * j + c, c % 2
                dve.wait_ge(mask_loaded[par], 16 * (j + c // 2 + 1))
                after(dve, logits_ready, PAIRS * HALVES * (g - 1))
                nc.vector.tensor_scalar(mask_add[par][:, :, 0:S], mask_raw[par][:, :, :], 0.0, BIG,
                                        ALU.is_equal, ALU.mult).then_inc(mask_ready, 1)

            def gate(i):
                step = GATE_STEPS * (i - 1)
                dve.wait_ge(gate_exp_done, i)
                nc.vector.tensor_scalar(g_one[:, :, :], g_exp[:, :, :], 1.0, None, ALU.add).then_inc(gate_step, 1)
                dve.wait_ge(gate_step, step + 1)
                nc.vector.reciprocal(g_score[:, :, :], g_one[:, :, :]).then_inc(gate_step, 1)
                dve.wait_ge(gate_step, step + 2)
                other = g_score[:, :, :].unsqueeze(2).broadcast_to([P, TT, E, E])
                own = g_score[:, :, :].unsqueeze(3).broadcast_to([P, TT, E, E])
                nc.vector.tensor_tensor(g_gt[:, :, :, :], other, own, ALU.is_gt).then_inc(gate_step, 1)
                nc.vector.tensor_tensor(g_eq[:, :, :, :], other, own, ALU.is_equal).then_inc(gate_step, 1)
                dve.wait_ge(gate_step, step + 4)
                nc.vector.tensor_tensor(g_tie[:, :, :, :], g_eq[:, :, :, :],
                                        before[:, :, :].unsqueeze(1).broadcast_to([P, TT, E, E]),
                                        ALU.mult).then_inc(gate_step, 1)
                dve.wait_ge(gate_step, step + 5)
                nc.vector.tensor_tensor(g_ahead[:, :, :, :], g_gt[:, :, :, :], g_tie[:, :, :, :],
                                        ALU.add).then_inc(gate_step, 1)
                dve.wait_ge(gate_step, step + 6)
                nc.vector.reduce_sum(g_rank[:, :, :], g_ahead[:, :, :, :], AX.X).then_inc(gate_step, 1)
                dve.wait_ge(gate_step, step + 7)
                nc.vector.scalar_tensor_tensor(g_keep[:, :, :], g_rank[:, :, :], 2.0, g_score[:, :, :],
                                               ALU.is_lt, ALU.mult).then_inc(gate_step, 1)
                dve.wait_ge(gate_step, step + 8)
                nc.vector.reduce_sum(g_sum[:, :], g_keep[:, :, :], AX.X).then_inc(gate_step, 1)
                dve.wait_ge(gate_step, step + 9)
                nc.vector.reciprocal(g_rsum[:, :], g_sum[:, :]).then_inc(gate_step, 1)
                dve.wait_ge(gate_step, step + 10)
                nc.vector.tensor_tensor(g_dense[:, :, :], g_keep[:, :, :],
                                        g_rsum[:, :].unsqueeze(2).broadcast_to([P, TT, E]), ALU.mult).then_inc(gate_step, 1)
                dve.wait_ge(gate_step, step + 11)
                after(dve, denseT_in_psum, i - 1)
                nc.vector.tensor_copy(g_parts[:, :, 0, :].bitcast(f32r), g_dense[:, :, :]).then_inc(gate_step, 1)
                dve.wait_ge(gate_step, step + 12)
                nc.vector.tensor_tensor(g_parts[:, :, 1, :].bitcast(f32r), g_dense[:, :, :], g_parts[:, :, 0, :],
                                        ALU.subtract).then_inc(gate_step, 1)

            def frame(j, p):
                i = 2 * j + p
                for k in range(HALVES):
                    e = HALVES * i + k
                    prev = has(j, p, 0, NG - 1) if k else has(j, p, 1, NG)
                    kp = (k - 1) % HALVES
                    par = p if k else (p + 1) % 2
                    if prev:
                        dve.wait_ge(pT_hi_ready, e)
                        after(dve, C_in_psum, e - 2)
                        nc.vector.tensor_tensor(pT_lo[kp % 2][:, :], PT_ps[:, :], pT_hi[kp % 2][:, :].bitcast(fp32),
                                                ALU.subtract).then_inc(pT_lo_ready, 1)
                    if has(j, p, 0, NG - 1):
                        dve.wait_ge(S_in_psum, e + 1)
                        if k == 0:
                            dve.wait_ge(mask_ready, i + 1)
                        after(dve, exp_done, PAIRS * (e - 1))
                        hold_waits(dve)
                        for r in range(PAIRS):
                            nc.vector.tensor_tensor_reduce(
                                out=logits[k % 2][:, r, :], in0=S_ps[:, P * r:P * (r + 1)], in1=mask_add[p][:, k % 4, :],
                                scale=1.0, scalar=3.0e38, op0=ALU.add, op1=ALU.min,
                                accum_out=neg_max[k % 2][:, r:r + 1]).then_inc(logits_ready, 1)
                    if k == 0 and has(j, p, -1, NG - 2):
                        par1 = (p + 1) % 2
                        dve.wait_ge(kv_loaded[par1], 32 * (j + (p + 1) // 2 + 1))
                        after(dve, kv_mv_done, i + 1)
                        for b in range(GB):
                            last = nc.vector.bn_stats(kv_bn[:, b, :], kv_raw[par1][:, b, :])
                        last.then_inc(kv_bn_done, 1)
                        dve.wait_ge(kv_bn_done, i + 2)
                        after(dve, kv_step, KV_STEPS * i + 3)
                        hold_waits(dve)
                        for b in range(GB):
                            last = nc.vector.bn_aggr(kv_mv[:, b, :], kv_bn[:, b, :])
                        last.then_inc(kv_mv_done, 1)
                    if k == 3 and has(j, p, -1, NG - 2):
                        par1 = (p + 1) % 2
                        dve.wait_ge(latT_hi_ready, i + 2)
                        after(dve, t_in_psum, HALVES * i)
                        nc.vector.tensor_tensor(latT_lo[par1][:, :, :],
                                                X_ps[:, :].rearrange("p (b f) -> p b f", b=GB)[:, :, S:P],
                                                latT_hi[par1][:, :, :].bitcast(fp32), ALU.subtract).then_inc(latT_lo_ready, 1)
                        convert_mask(j, p + 1)
                    if k == 0 and has(j, p, 2, NG + 1):
                        dve.wait_ge(denseT_in_psum, i - 1)
                        after(dve, H_in_psum, HT * (i - 2))
                        nc.vector.tensor_copy(denseT[:, :], X_ps[0:2 * E, 0:GT]).then_inc(denseT_ready, 1)
                    if prev:
                        dve.wait_ge(cT_hi_ready, e)
                        if kp == 0:
                            after(dve, W_in_psum, i - 1)
                        hs = slice(8 * (kp // 4), 8 * (kp // 4) + 8)
                        nc.vector.tensor_tensor(cT_lo[par][:, hs, kp % 4, :], C_ps[:, :].rearrange("p (h q) -> p h q", h=8),
                                                cT_hi[par][:, hs, kp % 4, :].bitcast(fp32),
                                                ALU.subtract).then_inc(cT_lo_ready, 1)
                    if has(j, p, 0, NG - 1):
                        dve.wait_ge(exp_done, PAIRS * (e + 1))
                        after(dve, probs_ready, e - 1)
                        nc.vector.reciprocal(rdenom[k % 2][:, :], denom[k % 2][:, :]).then_inc(rdenom_ready, 1)
                    if k == 5 and has(j, p, 1, NG):
                        par1, step = (p + 1) % 2, 3 * (i - 1)
                        dve.wait_ge(attn_in_psum, i)
                        dve.wait_ge(x_res_loaded[par1], 16 * (j + (p - 1) // 2 + 1))
                        after(dve, out_ready, TT * (i - 2))
                        nc.vector.tensor_tensor(x1[par1][:, :, :], X_ps[:, 0:GT].rearrange("p (t d) -> p t d", t=TT),
                                                x_res[par1][:, :, :], ALU.add).then_inc(x1_step, 1)
                        dve.wait_ge(x1_step, step + 1)
                        for t in range(TT):
                            last = nc.vector.bn_stats(x1_bn[:, t, :], x1[par1][:, t, :])
                        last.then_inc(x1_step, 1)
                        dve.wait_ge(x1_step, step + 2)
                        after(dve, x2_step, step)
                        hold_waits(dve)
                        for t in range(TT):
                            last = nc.vector.bn_aggr(x1_mv[:, t, :], x1_bn[:, t, :])
                        last.then_inc(x1_step, 1)
                    if k == 6 and has(j, p, 1, NG):
                        dve.wait_ge(x2T_hi_ready, i)
                        after(dve, H_in_psum, HT * (i - 1))
                        nc.vector.tensor_tensor(x2T_lo[:, :], X_ps[:, 0:GT], x2T_hi[:, :].bitcast(fp32),
                                                ALU.subtract).then_inc(x2T_lo_ready, 1)
                    if k in (6, 7) and has(j, p, 2, NG + 1):
                        t = k - 6
                        dve.wait_ge(y_in_psum, TT * (i - 2) + t + 1)
                        after(dve, out_stored[p], 16 * (j - 1))
                        nc.vector.tensor_tensor(out_sb[p][:, t, :], Y_ps[:, 256 * t:256 * t + D], x1[p][:, t, :],
                                                ALU.add).then_inc(out_ready, 1)
                    if k == 7 and has(j, p, 1, NG):
                        gate(i)
                    tile = ffn_tile(j, p, k)
                    if tile is not None:
                        r, n = tile
                        dve.wait_ge(tanh_done, n + 1)
                        after(dve, h_prod_done, n)
                        nc.vector.scalar_tensor_tensor(h_silu[:, :], h_tanh[:, :], 1.0, H_ps[:, 0:GT],
                                                       ALU.add, ALU.mult).then_inc(silu_done, 1)
                        dve.wait_ge(silu_done, n + 1)
                        if r == NT:
                            after(dve, y_in_psum, TT * (i - 1))
                            nc.vector.tensor_tensor(h[:, NT, :], h_silu[:, :], H_ps[:, 256:256 + GT],
                                                    ALU.mult).then_inc(h_prod_done, 1)
                        else:
                            after(dve, h_routed_done, NT * (i - 2) + r)
                            nc.vector.tensor_tensor(h_prod[:, :], h_silu[:, :], H_ps[:, 256:256 + GT],
                                                    ALU.mult).then_inc(h_prod_done, 1)
                            dve.wait_ge(h_prod_done, n + 1)
                            nc.vector.tensor_tensor(h[:, r, :], h_prod[:, :], Y_ps[:, 0:GT],
                                                    ALU.mult).then_inc(h_routed_done, 1)

            frames(dve, frame)

        @block.tensor
        def _(pe):
            pe.wait_ge(consts_ready, 1)
            pe.wait_ge(attn_w_loaded, 4 * 16)
            for n in range(6):
                src = (wq_raw, wk_raw, wv_raw)[n // 2]
                for c in range(4):
                    col = P * (4 * (n % 2) + c)
                    last = nc.tensor.transpose(banks[n][:, P * c:P * (c + 1)], src[:, col:col + P], ident[:, :])
                last.then_inc(wT_in_psum, 1)
            pe.wait_ge(wT_ready, 6)
            for n in range(2):
                for q in range(4):
                    for c in range(4):
                        hd = list(range(H))[bank_heads(q)][c]
                        rows = slice(DH * (hd % 2), DH * (hd % 2) + DH)
                        rhs = wT[1][rows, hd // 2, :] if n == 0 else wo_raw[rows, hd // 2, :]
                        last = nc.tensor.matmul(banks[4 * n + q][:, P * c:P * (c + 1)],
                                                wT[2 * n][rows, hd // 2, :], rhs, start=True, stop=True)
                    last.then_inc(MV_in_psum, 1)
            pe.wait_ge(V_evac, 4)
            pe.wait_ge(w_split, 8)
            pe.wait_ge(dve_consts, 5)
            pe.wait_ge(consts_ready, 2)

            def matmul3(dst, w_hi, w_lo, m_hi, m_lo, first=True, last=True):
                nc.tensor.matmul(dst, w_hi, m_hi, start=first, stop=False)
                nc.tensor.matmul(dst, w_hi, m_lo, start=False, stop=False)
                return nc.tensor.matmul(dst, w_lo, m_hi, start=False, stop=last)

            def frame(j, p):
                i = 2 * j + p
                for k in range(HALVES):
                    e = HALVES * i + k
                    prev = has(j, p, 0, NG - 1) if k else has(j, p, 1, NG)
                    kp = (k - 1) % HALVES
                    par, b = (p if k else (p + 1) % 2), kp % 4
                    if prev:
                        pe.wait_ge(probs_ready, e)
                        after(pe, pT_lo_ready, e - 1)
                        for r in range(PAIRS):
                            last = nc.tensor.transpose(PT_ps[:, P * r:P * (r + 1)], probs[kp % 2][:, r, :], ident[:, :])
                        last.then_inc(pT_in_psum, 1)
                    if has(j, p, 0, NG - 1):
                        if k == 0:
                            pe.wait_ge(kvT_ready, i + 1)
                        if k in (0, 4):
                            pe.wait_ge(t_ready, e + 4)
                        after(pe, logits_ready, PAIRS * e)
                        for r in range(PAIRS):
                            hd = 8 * (k // 4) + 2 * r
                            last = nc.tensor.matmul(S_ps[:, P * r:P * (r + 1)], tT[:, k % 4, hd:hd + 2, :],
                                                    kvT[p][:, k % 4, :], start=True, stop=True)
                        last.then_inc(S_in_psum, 1)
                    if k == 3 and has(j, p, -1, NG - 2):
                        pe.wait_ge(kv_step, KV_STEPS * (i + 1) + 5)
                        for b1 in range(GB):
                            last = nc.tensor.transpose(X_ps[:, P * b1:P * (b1 + 1)], kv_f[:, b1, :], ident[:, :])
                        last.then_inc(kvT_in_psum, 1)
                    if (has(j, p, 0, NG - 1) if k < 4 else has(j, p, -1, NG - 2)):
                        c, pl = (k + 4) % HALVES, (p if k < 4 else (p + 1) % 2)
                        if k == 4:
                            pe.wait_ge(latT_lo_ready, i + 2)
                        after(pe, t_ready, e + 4)
                        for n in range(2):
                            hd = 2 * c + n
                            last = matmul3(T_ps[:, GT * n:GT * (n + 1)], MV_hi[0][:, hd, :], MV_lo[0][:, hd, :],
                                           latT_hi[pl][:, :, :], latT_lo[pl][:, :, :])
                        last.then_inc(t_in_psum, 1)
                    if k == 0 and has(j, p, 2, NG + 1):
                        pe.wait_ge(gate_step, GATE_STEPS * (i - 1))
                        for t in range(TT):
                            last = nc.tensor.transpose(X_ps[0:2 * E, P * t:P * (t + 1)],
                                                       g_parts[:, t, :, :].rearrange("p a e -> p (a e)"), ident[:, :])
                        last.then_inc(denseT_in_psum, 1)
                    if prev:
                        pe.wait_ge(pT_lo_ready, e)
                        if kp == 0:
                            pe.wait_ge(kv_step, KV_STEPS * (i + 1))
                        after(pe, cT_lo_ready, e - 1)
                        matmul3(C_ps[:, :], kv_hi[par][:, b, :], kv_lo[par][:, b, :], pT_hi[kp % 2][:, :],
                                pT_lo[kp % 2][:, :]).then_inc(C_in_psum, 1)
                    if 1 <= k <= 4 and has(j, p, 1, NG):
                        if k == 1:
                            pe.wait_ge(cT_lo_ready, HALVES * i)
                            after(pe, attnT_ready, i - 1)
                        p1 = (p + 1) % 2
                        for hd in range(4 * (k - 1), 4 * k):
                            last = matmul3(W_ps[:, 0:GT], MV_hi[1][:, hd, :], MV_lo[1][:, hd, :],
                                           cT_hi[p1][:, hd, :, :], cT_lo[p1][:, hd, :, :],
                                           first=hd == 0, last=hd == H - 1)
                        if k == 4:
                            last.then_inc(W_in_psum, 1)
                    if k == 5 and has(j, p, 1, NG):
                        pe.wait_ge(attnT_ready, i)
                        if has(j, p, -1, NG - 2):
                            pe.wait_ge(latT_lo_ready, i + 2)
                        for t in range(TT):
                            last = nc.tensor.transpose(X_ps[:, P * t:P * (t + 1)], attnT[:, P * t:P * (t + 1)], ident[:, :])
                        last.then_inc(attn_in_psum, 1)
                    if k == 6 and has(j, p, 1, NG):
                        pe.wait_ge(x2_step, 3 * i)
                        for t in range(TT):
                            last = nc.tensor.transpose(X_ps[:, P * t:P * (t + 1)], x2[:, t, :], ident[:, :])
                        last.then_inc(x2T_in_psum, 1)
                    if k in (6, 7) and has(j, p, 2, NG + 1):
                        t = k - 6
                        if t == 0:
                            pe.wait_ge(h_prod_done, HT * (i - 1))
                            pe.wait_ge(h_routed_done, NT * (i - 1))
                        else:
                            pe.wait_ge(out_ready, TT * (i - 2) + 1)
                        for n in range(HT):
                            last = nc.tensor.matmul(Y_ps[:, 256 * t:256 * t + D], h[:, n, P * t:P * (t + 1)],
                                                    w2_sb[:, n, :], start=n == 0, stop=n == HT - 1)
                        last.then_inc(y_in_psum, 1)
                    if k == 7 and has(j, p, 1, NG):
                        pe.wait_ge(x2T_ready, i)
                        pe.wait_ge(x2T_lo_ready, i)
                        for t in range(TT):
                            last = nc.tensor.matmul(X_ps[:, E * t:E * (t + 1)], x2T[:, P * t:P * (t + 1)], gate_sb[:, :],
                                                    start=True, stop=True)
                        last.then_inc(gate_in_psum, 1)
                    tile = ffn_tile(j, p, k)
                    if tile is not None:
                        r, n = tile
                        if r != NT:
                            if r == 0:
                                pe.wait_ge(denseT_ready, i - 1)
                                after(pe, out_ready, TT * (i - 2))
                            after(pe, h_routed_done, NT * (i - 2) + r)
                            nc.tensor.matmul(Y_ps[:, 0:GT], expert_rows_r[:, r, :, :].rearrange("p e f -> p (e f)"),
                                             denseT[:, :], start=True, stop=True)
                        after(pe, h_prod_done, n)
                        for a in range(2):
                            last = matmul3(H_ps[:, 256 * a:256 * a + GT], w13_hi[:, a, r, :], w13_lo[:, a, r, :],
                                           x2T_hi[:, :], x2T_lo[:, :])
                        last.then_inc(H_in_psum, 1)

            frames(pe, frame)


_INS = ['x', 'ctx_1024', 'mask_BxS2_ik0', 'L0_xattn_ln_m_w', 'L0_xattn_ln_m_b', 'L0_xattn_ln_l_w', 'L0_xattn_ln_l_b',
        'L0_xattn_Wq', 'L0_xattn_Wk', 'L0_xattn_Wv', 'L0_xattn_Wo', 'L0_ffn_gate_w', 'L0_ffn_w1', 'L0_ffn_w3',
        'L0_ffn_w2', 'L0_ffn_ws1', 'L0_ffn_ws3', 'L0_ffn_ws2']


def kernel(**inputs):
    import numpy as _np
    import concourse.bacc as _bacc
    from concourse import mybir as _mybir
    from concourse.bass_utils import run_bass_kernel_spmd as _run

    nc = _bacc.Bacc("TRN2", target_bir_lowering=False, num_devices=1)
    arrays, args = {}, []
    for name in _INS:
        a = _np.ascontiguousarray(inputs[name])
        arrays[f"in_{name}"] = a
        args.append(nc.dram_tensor(f"in_{name}", a.shape, _mybir.dt.from_np(a.dtype), kind="ExternalInput").ap())
    out = nc.dram_tensor("out_0", arrays["in_x"].shape, _mybir.dt.float32, kind="ExternalOutput").ap()
    xattn_moe_ffn_kernel(nc, *args, out)
    r = _run(nc, [arrays], core_ids=[0])
    return r.results[0]["out_0"]
```

```python
import concourse.bass as bass
from concourse import mybir
from contextlib import ExitStack


def xattn_moe_ffn_kernel(nc, x, ctx, mask, ln_m_w, ln_m_b, ln_l_w, ln_l_b, Wq, Wk, Wv, Wo,
                         gate_w, w1, w3, w2, ws1, ws3, ws2, out):
    fp32 = mybir.dt.float32
    f32r = mybir.dt.float32r
    ALU = mybir.AluOpType
    ACT = mybir.ActivationFunctionType
    AX = mybir.AxisListType

    P = 128
    B, S, D = x.shape
    INNER = Wq.shape[1]
    DH = 64
    H = INNER // DH
    E, _, FH = w1.shape
    EPS = 1e-5
    SCALE = float(DH) ** -0.5
    BIG = 1e30
    GB = 4
    NG = B // GB
    GT = GB * S
    HALVES = 2 * GB
    PAIRS = 4
    NT = E * FH // P
    TT = GT // P

    es = ExitStack()
    with es:
        def sb(name, shape, dt=fp32):
            return es.enter_context(nc.sbuf_tensor(name, shape, dt))

        def sem(name):
            return es.enter_context(nc.semaphore(name))

        MV_hi = [sb(f"MV_hi{n}", [P, H, D], f32r) for n in range(2)]
        MV_lo = [sb(f"MV_lo{n}", [P, H, D], f32r) for n in range(2)]
        w13_hi = sb("w13_hi", [P, 2, NT + 1, P], f32r)
        w13_lo = sb("w13_lo", [P, 2, NT + 1, P], f32r)
        w2_sb = sb("w2_sb", [P, NT + 1, D])
        gate_sb = sb("gate_sb", [P, E])
        ln_w_bc = sb("ln_w_bc", [P, D])
        ln_b_bc = sb("ln_b_bc", [P, D])
        ident = sb("ident", [P, P])
        expert_rows = sb("expert_rows", [2 * E, NT, 2, FH])
        expert_rows_r = sb("expert_rows_r", [2 * E, NT, 2, FH], f32r)
        before = sb("before", [P, E, E])
        var_mul = sb("var_mul", [P, 1])
        var_add = sb("var_add", [P, 1])
        minus_half = sb("minus_half", [P, GB])
        eps_col = sb("eps_col", [P, 1])

        kv_raw = [sb(f"kv_raw{n}", [P, GB, D]) for n in range(2)]
        kv_bn = sb("kv_bn", [P, GB, 6])
        kv_mv = sb("kv_mv", [P, GB, 2])
        kv_ve = sb("kv_ve", [P, GB])
        kv_r = sb("kv_r", [P, GB])
        kv_n = sb("kv_n", [P, GB, D])
        kv_nw = sb("kv_nw", [P, GB, D])
        kv_f = sb("kv_f", [P, GB, D])
        kv_hi = [sb(f"kv_hi{n}", [P, GB, D], f32r) for n in range(2)]
        kv_lo = [sb(f"kv_lo{n}", [P, GB, D], f32r) for n in range(2)]
        kvT = [sb(f"kvT{n}", [P, GB, P]) for n in range(2)]
        latT_hi = [sb(f"latT_hi{n}", [P, GB, S], f32r) for n in range(2)]
        latT_lo = [sb(f"latT_lo{n}", [P, GB, S], f32r) for n in range(2)]
        tT = sb("tT", [P, GB, H, S])
        mask_raw = [sb(f"mask_raw{n}", [P, GB, S], mybir.dt.int32) for n in range(2)]
        mask_add = [sb(f"mask_add{n}", [P, GB, P]) for n in range(2)]
        logits = [sb(f"logits{n}", [P, PAIRS, P]) for n in range(2)]
        neg_max = [sb(f"neg_max{n}", [P, PAIRS]) for n in range(2)]
        probs = [sb(f"probs{n}", [P, PAIRS, P]) for n in range(4)]
        denom = [sb(f"denom{n}", [P, PAIRS]) for n in range(4)]
        rdenom = [sb(f"rdenom{n}", [P, PAIRS]) for n in range(4)]
        pT_hi = [sb(f"pT_hi{n}", [P, PAIRS * P], f32r) for n in range(2)]
        pT_lo = [sb(f"pT_lo{n}", [P, PAIRS * P], f32r) for n in range(2)]
        attnT = sb("attnT", [P, GT])
        x_res = [sb(f"x_res{n}", [P, TT, D]) for n in range(2)]
        x1 = [sb(f"x1_{n}", [P, TT, D]) for n in range(2)]
        x1_bn = sb("x1_bn", [P, TT, 6])
        x1_mv = sb("x1_mv", [P, TT, 2])
        x1_ve = sb("x1_ve", [P, TT])
        x1_r = sb("x1_r", [P, TT])
        x2 = sb("x2", [P, TT, D])
        x2T = sb("x2T", [P, GT])
        x2T_hi = sb("x2T_hi", [P, GT], f32r)
        x2T_lo = sb("x2T_lo", [P, GT], f32r)
        g_exp = sb("g_exp", [P, TT, E])
        g_one = sb("g_one", [P, TT, E])
        g_score = sb("g_score", [P, TT, E])
        g_gt = sb("g_gt", [P, TT, E, E])
        g_eq = sb("g_eq", [P, TT, E, E])
        g_tie = sb("g_tie", [P, TT, E, E])
        g_ahead = sb("g_ahead", [P, TT, E, E])
        g_rank = sb("g_rank", [P, TT, E])
        g_keep = sb("g_keep", [P, TT, E])
        g_sum = sb("g_sum", [P, TT])
        g_rsum = sb("g_rsum", [P, TT])
        g_dense = sb("g_dense", [P, TT, E])
        g_parts = sb("g_parts", [P, TT, 2, E])
        denseT = sb("denseT", [2 * E, GT], f32r)
        h_tanh = sb("h_tanh", [P, GT])
        h_silu = sb("h_silu", [P, GT])
        h_prod = sb("h_prod", [P, GT])
        h = sb("h", [P, NT + 1, GT])
        out_sb = [sb(f"out_sb{n}", [P, TT, D]) for n in range(2)]

        with ExitStack() as setup_only:
            def su(name, shape):
                return setup_only.enter_context(nc.sbuf_tensor(name, shape, fp32))

            wq_raw = su("wq_raw", [P, INNER])
            wk_raw = su("wk_raw", [P, INNER])
            wv_raw = su("wv_raw", [P, INNER])
            wo_raw = su("wo_raw", [P, H // 2, D])
            wT = [su(f"wT{n}", [P, H // 2, D]) for n in range(3)]
            w13_stage = [su(f"w13_stage{n}", [P, (NT + 1) * P]) for n in range(2)]
        cT_hi = [sb(f"cT_hi{n}", [P, H, GB, S], f32r) for n in range(2)]
        cT_lo = [sb(f"cT_lo{n}", [P, H, GB, S], f32r) for n in range(2)]

        banks = [es.enter_context(nc.psum_tensor(f"bank{n}", [P, 512], fp32)) for n in range(8)]
        S_ps, PT_ps, C_ps, T_ps, W_ps, H_ps, X_ps, Y_ps = banks

        kv_loaded = [sem(f"kv_loaded{n}") for n in range(2)]
        mask_loaded = [sem(f"mask_loaded{n}") for n in range(2)]
        x_res_loaded = [sem(f"x_res_loaded{n}") for n in range(2)]
        attn_w_loaded = sem("attn_w_loaded")
        ffn_w_loaded = sem("ffn_w_loaded")
        ln_w_loaded = sem("ln_w_loaded")
        out_stored = [sem(f"out_stored{n}") for n in range(2)]
        waits_held = sem("waits_held")
        const_set = sem("const_set")
        consts_ready = sem("consts_ready")
        dve_consts = sem("dve_consts")
        wT_in_psum = sem("wT_in_psum")
        wT_ready = sem("wT_ready")
        MV_in_psum = sem("MV_in_psum")
        MV_hi_ready = sem("MV_hi_ready")
        MV_lo_ready = sem("MV_lo_ready")
        kv_bn_done = sem("kv_bn_done")
        kv_mv_done = sem("kv_mv_done")
        kv_step = sem("kv_step")
        kvT_in_psum = sem("kvT_in_psum")
        kvT_ready = sem("kvT_ready")
        latT_hi_ready = sem("latT_hi_ready")
        latT_lo_ready = sem("latT_lo_ready")
        t_in_psum = sem("t_in_psum")
        t_ready = sem("t_ready")
        mask_ready = sem("mask_ready")
        S_in_psum = sem("S_in_psum")
        logits_ready = sem("logits_ready")
        exp_done = sem("exp_done")
        rdenom_ready = sem("rdenom_ready")
        probs_ready = sem("probs_ready")
        pT_in_psum = sem("pT_in_psum")
        pT_hi_ready = sem("pT_hi_ready")
        pT_lo_ready = sem("pT_lo_ready")
        C_in_psum = sem("C_in_psum")
        cT_hi_ready = sem("cT_hi_ready")
        cT_lo_ready = sem("cT_lo_ready")
        W_in_psum = sem("W_in_psum")
        attnT_ready = sem("attnT_ready")
        attn_in_psum = sem("attn_in_psum")
        x1_step = sem("x1_step")
        x2_step = sem("x2_step")
        x2T_in_psum = sem("x2T_in_psum")
        x2T_ready = sem("x2T_ready")
        x2T_hi_ready = sem("x2T_hi_ready")
        x2T_lo_ready = sem("x2T_lo_ready")
        gate_in_psum = sem("gate_in_psum")
        gate_exp_done = sem("gate_exp_done")
        gate_step = sem("gate_step")
        denseT_in_psum = sem("denseT_in_psum")
        denseT_ready = sem("denseT_ready")
        H_in_psum = sem("H_in_psum")
        tanh_done = sem("tanh_done")
        silu_done = sem("silu_done")
        h_prod_done = sem("h_prod_done")
        h_routed_done = sem("h_routed_done")
        y_in_psum = sem("y_in_psum")
        out_ready = sem("out_ready")

        GATE_STEPS = 13
        KV_STEPS = 8
        X2_STEPS = 4
        PROJ_HEADS = (0, 2, 4, 6, 8, 12, 16)
        HT = NT + 1

        block = es.enter_context(nc.Block())

        def after(eng, semaphore, count):
            if not isinstance(count, int) or count > 0:
                eng.wait_ge(semaphore, count)

        def frames(eng, frame):
            for i in range(-2, 4):
                frame(i // 2, i % 2)
            with eng.Fori(2, NG // 2 - 1) as j:
                frame(j, 0)
                frame(j, 1)
            for i in range(NG - 2, NG + 3):
                frame(i // 2, i % 2)

        def has(j, c, first, last):
            return not isinstance(j, int) or first <= 2 * j + c <= last

        def bank_heads(q):
            return slice(8 * (q // 2) + q % 2, 8 * (q // 2) + 8, 2)

        def hold_waits(eng):
            eng.sem_inc(waits_held, 1)

        def has_half(j, p, k, lag):
            return has(j, p, 0, NG - 1) if k >= lag else has(j, p, 1, NG)

        def half_buffers(p, k, lag):
            return (k - lag) % HALVES, (p if k >= lag else 1 - p)

        def query_chunk(j, p, k):
            ahead = 1 if k >= 3 else 0
            return ((k + 5) % HALVES, ahead) if has(j, p, -ahead, NG - 1 - ahead) else None

        def query_chunk_before(j, p, k):
            if k == 0:
                return (4, 0) if has(j, p, 0, NG - 1) else None
            return query_chunk(j, p, k - 1)

        def ffn_tile(j, p, k):
            i = 2 * j + p
            if not has(j, p, 2, NG + 1):
                return None
            if k == 1:
                return NT, HT * (i - 2)
            return (k - 3, HT * (i - 2) + k - 2) if 3 <= k <= 6 else None

        @block.sync
        def _(sp):
            def load_kv(j, c):
                g, par = 2 * j + c, c % 2
                half = j + c // 2
                after(sp, kv_step, KV_STEPS * (g - 2) + 3)
                sp.dma_start(kv_raw[par][0:S, :, :], ctx[bass.ds(GB * g, GB), :, :].rearrange("b s d -> s b d")
                             ).then_inc(kv_loaded[par], 16)
                sp.dma_start(kv_raw[par][S:P, :, :], x[bass.ds(GB * g, GB), :, :].rearrange("b s d -> s b d")
                             ).then_inc(kv_loaded[par], 16)
                after(sp, mask_ready, g - 1)
                sp.dma_start(mask_raw[par][:, :, :], mask[bass.ds(GB * g, GB), :].partition_broadcast(P)
                             ).then_inc(mask_loaded[par], 16)

            load_kv(0, 0)
            for dst, src in ((wq_raw, Wq), (wk_raw, Wk), (wv_raw, Wv)):
                sp.dma_start(dst[:, :], src).then_inc(attn_w_loaded, 16)
            sp.dma_start(wo_raw[:, :, :], Wo.rearrange("(c p) n -> p c n", p=P)).then_inc(attn_w_loaded, 16)
            for dst, m, l in ((ln_w_bc, ln_m_w, ln_l_w), (ln_b_bc, ln_m_b, ln_l_b)):
                sp.dma_start(dst[0:S, :], m.partition_broadcast(S)).then_inc(ln_w_loaded, 16)
                sp.dma_start(dst[S:P, :], l.partition_broadcast(S)).then_inc(ln_w_loaded, 16)
            for n, (w, ws) in enumerate(((w1, ws1), (w3, ws3))):
                stage = w13_stage[n]
                sp.dma_start(stage[:, 0:NT * P].rearrange("p (e f) -> p e f", e=E),
                             w.rearrange("e d f -> d e f")).then_inc(ffn_w_loaded, 16)
                sp.dma_start(stage[:, NT * P:HT * P], ws).then_inc(ffn_w_loaded, 16)
            sp.dma_start(w2_sb[:, 0:NT, :], w2.rearrange("(i e) f d -> (e f) i d", e=2)).then_inc(ffn_w_loaded, 16)
            sp.dma_start(w2_sb[:, NT, :], ws2).then_inc(ffn_w_loaded, 16)
            sp.dma_start(gate_sb[:, :], gate_w).then_inc(ffn_w_loaded, 16)

            def frame(j, p):
                i = 2 * j + p
                if has(j, p, -1, NG - 3):
                    load_kv(j, p + 2)
                if has(j, p, 0, NG - 1):
                    after(sp, x1_step, 3 * (i - 2) + 1)
                    sp.dma_start(x_res[p][:, :, :],
                                 x.rearrange("b s d -> (b s) d")[bass.ds(GT * i, GT), :].rearrange("(t q) d -> q t d", q=P)
                                 ).then_inc(x_res_loaded[p], 16)
                if has(j, p, 3, NG + 2):
                    after(sp, out_ready, i - 2)
                    sp.dma_start(out.rearrange("b s d -> (b s) d")[bass.ds(GT * (i - 3), GT), :].rearrange("(t q) d -> q t d", q=P),
                                 out_sb[1 - p][:, :, :]).then_inc(out_stored[1 - p], 16)

            frames(sp, frame)
            for n in range(2):
                sp.wait_ge(out_stored[n], 16 * (NG // 2))

        @block.gpsimd
        def _(pool):
            for n, (ap, value) in enumerate((
                    (ident[:, :], 0.0), (expert_rows[:, :, :, :], 0.0), (before[:, :, :], 1.0),
                    (var_mul[0:S, :], 1.0), (var_mul[S:P, :], 1.0 + EPS),
                    (var_add[0:S, :], EPS), (var_add[S:P, :], EPS * EPS),
                    (minus_half[:, :], -0.5), (eps_col[:, :], EPS),
                    (mask_add[0][:, :, :], 0.0), (mask_add[1][:, :, :], 0.0))):
                nc.gpsimd.memset(ap, value).then_inc(const_set, 1)
                pool.wait_ge(const_set, n + 1)
            nc.gpsimd.affine_select(out=ident[:, :], in_=ident[:, :], compare_op=ALU.not_equal, fill=1.0,
                                    base=0, pattern=[[-1, P]], channel_multiplier=1).then_inc(consts_ready, 1)
            nc.gpsimd.affine_select(out=expert_rows[:, :, :, :], in_=expert_rows[:, :, :, :],
                                    compare_op=ALU.not_equal, fill=1.0, base=0,
                                    pattern=[[-2, NT], [-1, 2], [0, FH]], channel_multiplier=1).then_inc(const_set, 1)
            pool.wait_ge(const_set, 12)
            nc.gpsimd.affine_select(out=expert_rows[:, :, :, :], in_=expert_rows[:, :, :, :],
                                    compare_op=ALU.not_equal, fill=1.0, base=-E,
                                    pattern=[[-2, NT], [-1, 2], [0, FH]], channel_multiplier=1).then_inc(const_set, 1)
            nc.gpsimd.affine_select(out=before[:, :, :], in_=before[:, :, :], compare_op=ALU.is_gt, fill=0.0,
                                    base=0, pattern=[[1, E], [-1, E]], channel_multiplier=0).then_inc(const_set, 1)
            pool.wait_ge(const_set, 14)
            nc.gpsimd.tensor_copy(expert_rows_r[:, :, :, :], expert_rows[:, :, :, :]).then_inc(consts_ready, 1)

            def keys(j, c, steps):
                g, par = 2 * j + c, c % 2
                step = KV_STEPS * g
                if 1 in steps:
                    pool.wait_ge(kv_mv_done, g + 1)
                    hold_waits(pool)
                    nc.gpsimd.tensor_scalar(kv_ve[:, :], kv_mv[:, :, 1], var_mul[:, 0:1], var_add[:, 0:1],
                                            ALU.mult, ALU.add).then_inc(kv_step, 1)
                    pool.wait_ge(kv_step, step + 1)
                    nc.gpsimd.tensor_tensor(kv_r[:, :], kv_ve[:, :], minus_half[:, :], ALU.pow).then_inc(kv_step, 1)
                if 3 in steps:
                    pool.wait_ge(kv_step, step + 2)
                    nc.gpsimd.tensor_tensor(kv_n[:, :, :], kv_raw[par][:, :, :],
                                            kv_mv[:, :, 0].unsqueeze(2).broadcast_to([P, GB, D]),
                                            ALU.subtract).then_inc(kv_step, 1)
                if 4 in steps:
                    pool.wait_ge(kv_step, step + 3)
                    nc.gpsimd.tensor_tensor(kv_n[:, :, :], kv_n[:, :, :], kv_r[:, :].unsqueeze(2).broadcast_to([P, GB, D]),
                                            ALU.mult).then_inc(kv_step, 1)
                if 5 in steps:
                    pool.wait_ge(kv_step, step + 4)
                    if isinstance(j, int) and g == 0:
                        pool.wait_ge(ln_w_loaded, 64)
                    nc.gpsimd.tensor_tensor(kv_nw[:, :, :], kv_n[:, :, :],
                                            ln_w_bc[:, :].unsqueeze(1).broadcast_to([P, GB, D]), ALU.mult).then_inc(kv_step, 1)
                if 6 in steps:
                    pool.wait_ge(kv_step, step + 5)
                    after(pool, kvT_in_psum, g)
                    nc.gpsimd.tensor_tensor(kv_f[:, :, :], kv_nw[:, :, :],
                                            ln_b_bc[:, :].unsqueeze(1).broadcast_to([P, GB, D]), ALU.add).then_inc(kv_step, 1)
                if 7 in steps:
                    after(pool, C_in_psum, HALVES * (g - 1))
                    pool.wait_ge(kv_step, step + 6)
                    hold_waits(pool)
                    nc.gpsimd.tensor_copy(kv_hi[par][:, :, :], kv_f[:, :, :]).then_inc(kv_step, 1)
                if 8 in steps:
                    pool.wait_ge(kv_step, step + 7)
                    nc.gpsimd.tensor_tensor(kv_lo[par][:, :, :], kv_f[:, :, :], kv_hi[par][:, :, :].bitcast(fp32),
                                            ALU.subtract).then_inc(kv_step, 1)

            def frame(j, p):
                i = 2 * j + p
                for k in range(HALVES):
                    e = HALVES * i + k
                    if has_half(j, p, k, 2):
                        n = (k - 2) % 4
                        pool.wait_ge(rdenom_ready, e - 1)
                        nc.gpsimd.tensor_tensor(probs[n][:, :, :], probs[n][:, :, :],
                                                rdenom[n][:, :].unsqueeze(2).broadcast_to([P, PAIRS, P]),
                                                ALU.mult).then_inc(probs_ready, 1)
                    if k == 7 and has(j, p, 1, NG):
                        step = X2_STEPS * (i - 1)
                        pool.wait_ge(x1_step, 3 * i)
                        hold_waits(pool)
                        nc.gpsimd.tensor_scalar(x1_ve[:, :], x1_mv[:, :, 1], 1.0, eps_col[:, 0:1],
                                                ALU.mult, ALU.add).then_inc(x2_step, 1)
                        pool.wait_ge(x2_step, step + 1)
                        nc.gpsimd.tensor_tensor(x1_r[:, :], x1_ve[:, :], minus_half[:, 0:TT],
                                                ALU.pow).then_inc(x2_step, 1)
                        after(pool, x2T_in_psum, i - 1)
                        nc.gpsimd.tensor_tensor(x2[:, :, :], x1[1 - p][:, :, :],
                                                x1_mv[:, :, 0].unsqueeze(2).broadcast_to([P, TT, D]),
                                                ALU.subtract).then_inc(x2_step, 1)
                        pool.wait_ge(x2_step, step + 3)
                        nc.gpsimd.tensor_tensor(x2[:, :, :], x2[:, :, :], x1_r[:, :].unsqueeze(2).broadcast_to([P, TT, D]),
                                                ALU.mult).then_inc(x2_step, 1)
                    if has(j, p, -1, NG - 2):
                        keys(j, p + 1, {0: (5,), 1: (6,), 4: (7,), 5: (8,)}.get(k, ()))
                    if has(j, p, -2, NG - 3):
                        keys(j, p + 2, {5: (1, 2), 6: (3,), 7: (4,)}.get(k, ()))

            frames(pool, frame)

        @block.scalar
        def _(act):
            for q in range(8):
                act.wait_ge(MV_in_psum, q + 1)
                nc.scalar.mul(MV_hi[q // 4][:, bank_heads(q % 4), :], banks[q][:, :].rearrange("p (h d) -> p h d", h=4),
                              -SCALE if q < 4 else 1.0).then_inc(MV_hi_ready, 1)

            def frame(j, p):
                i = 2 * j + p
                for k in range(HALVES):
                    e = HALVES * i + k
                    tile = ffn_tile(j, p, k - 1) if k else None
                    if tile is not None:
                        n = tile[1]
                        act.wait_ge(H_in_psum, n + 1)
                        after(act, silu_done, n)
                        nc.scalar.activation(h_tanh[:, :], H_ps[:, 0:GT], ACT.Tanh, scale=0.5).then_inc(tanh_done, 1)
                    chunk = query_chunk_before(j, p, k)
                    if chunk is not None:
                        c, ahead = chunk
                        act.wait_ge(t_in_psum, e + 5)
                        after(act, S_in_psum, HALVES * (i + ahead - 1) + (4 if c < 4 else 8))
                        nc.scalar.copy(tT[:, :, 2 * c:2 * c + 2, :].rearrange("p b h q -> p h b q"),
                                       T_ps[:, :].rearrange("p (h b q) -> p h b q", h=2, b=GB)).then_inc(t_ready, 1)
                    if has_half(j, p, k, 3):
                        n = (k - 3) % 2
                        act.wait_ge(pT_in_psum, e - 2)
                        after(act, C_in_psum, e - 4)
                        nc.scalar.copy(pT_hi[n][:, :], PT_ps[:, :]).then_inc(pT_hi_ready, 1)
                    if has_half(j, p, k, 4):
                        kl, par = half_buffers(p, k, 4)
                        act.wait_ge(C_in_psum, e - 3)
                        if kl == 0:
                            after(act, W_in_psum, i - 1)
                        nc.scalar.copy(cT_hi[par][:, 8 * (kl // 4):8 * (kl // 4) + 8, kl % 4, :],
                                       C_ps[:, :].rearrange("p (h q) -> p h q", h=8)).then_inc(cT_hi_ready, 1)
                    if k == 2 and has(j, p, 2, NG + 1):
                        act.wait_ge(gate_in_psum, i - 1)
                        after(act, gate_step, GATE_STEPS * (i - 3) + 1)
                        nc.scalar.activation(g_exp[:, :, :], X_ps[:, 0:TT * E].rearrange("p (t e) -> p t e", e=E),
                                             ACT.Exp, scale=-1.0).then_inc(gate_exp_done, 1)
                    if k == 6 and has(j, p, 1, NG):
                        act.wait_ge(W_in_psum, i)
                        after(act, attn_in_psum, i - 1)
                        nc.scalar.copy(attnT[:, :], W_ps[:, 0:GT]).then_inc(attnT_ready, 1)
                    if k == 1 and has(j, p, 2, NG + 1):
                        act.wait_ge(x2T_in_psum, i - 1)
                        after(act, gate_in_psum, i - 2)
                        nc.scalar.copy(x2T[:, :], X_ps[:, 0:GT]).then_inc(x2T_ready, 1)
                        after(act, H_in_psum, HT * (i - 2))
                        nc.scalar.copy(x2T_hi[:, :], X_ps[:, 0:GT]).then_inc(x2T_hi_ready, 1)
                    if has_half(j, p, k, 1):
                        n = k - 1
                        for r in range(PAIRS):
                            act.wait_ge(logits_ready, PAIRS * (e - 1) + r + 1)
                            if r == 0:
                                after(act, pT_in_psum, e - 4)
                            nc.scalar.activation(probs[n % 4][:, r, :], logits[n % 2][:, r, :], ACT.Exp,
                                                 bias=neg_max[n % 2][:, r:r + 1], scale=-1.0,
                                                 accum_out=denom[n % 4][:, r:r + 1]).then_inc(exp_done, 1)
                    if k == 2 and has(j, p, -1, NG - 2):
                        act.wait_ge(kvT_in_psum, i + 2)
                        after(act, S_in_psum, HALVES * i)
                        nc.scalar.copy(kvT[1 - p][:, :, :], X_ps[:, :].rearrange("p (b f) -> p b f", b=GB)
                                       ).then_inc(kvT_ready, 1)
                        after(act, t_in_psum, HALVES * i)
                        nc.scalar.copy(latT_hi[1 - p][:, :, :],
                                       X_ps[:, :].rearrange("p (b f) -> p b f", b=GB)[:, :, S:P]
                                       ).then_inc(latT_hi_ready, 1)

            frames(act, frame)

        @block.vector
        def _(dve):
            for n in range(6):
                dve.wait_ge(wT_in_psum, n + 1)
                nc.vector.tensor_copy(wT[n // 2][:, 4 * (n % 2):4 * (n % 2) + 4, :],
                                      banks[n][:, :].rearrange("p (c d) -> p c d", c=4)).then_inc(wT_ready, 1)
            for q in range(8):
                dve.wait_ge(MV_hi_ready, q + 1)
                heads = bank_heads(q % 4)
                nc.vector.scalar_tensor_tensor(MV_lo[q // 4][:, heads, :], banks[q][:, :].rearrange("p (h d) -> p h d", h=4),
                                               -SCALE if q < 4 else 1.0, MV_hi[q // 4][:, heads, :].bitcast(fp32),
                                               ALU.mult, ALU.subtract).then_inc(MV_lo_ready, 1)
            dve.wait_ge(ffn_w_loaded, 7 * 16)
            for n in range(2):
                nc.vector.tensor_copy(w13_hi[:, n, :, :],
                                      w13_stage[n][:, :].rearrange("p (t f) -> p t f", f=P)).then_inc(dve_consts, 1)
            nc.vector.tensor_scalar(w2_sb[:, :, :], w2_sb[:, :, :], 0.5, None, ALU.mult).then_inc(dve_consts, 1)
            dve.wait_ge(dve_consts, 3)
            for n in range(2):
                nc.vector.tensor_tensor(w13_lo[:, n, :, :], w13_stage[n][:, :].rearrange("p (t f) -> p t f", f=P),
                                        w13_hi[:, n, :, :].bitcast(fp32), ALU.subtract).then_inc(dve_consts, 1)
            dve.wait_ge(const_set, 14)
            dve.wait_ge(dve_consts, 5)

            def convert_mask(j, c):
                g, par = 2 * j + c, c % 2
                dve.wait_ge(mask_loaded[par], 16 * (j + c // 2 + 1))
                after(dve, logits_ready, PAIRS * HALVES * (g - 1))
                nc.vector.tensor_scalar(mask_add[par][:, :, 0:S], mask_raw[par][:, :, :], 0.0, BIG,
                                        ALU.is_equal, ALU.mult).then_inc(mask_ready, 1)

            def gate(i):
                step = GATE_STEPS * (i - 1)
                dve.wait_ge(gate_exp_done, i)
                nc.vector.tensor_scalar(g_one[:, :, :], g_exp[:, :, :], 1.0, None, ALU.add).then_inc(gate_step, 1)
                dve.wait_ge(gate_step, step + 1)
                nc.vector.reciprocal(g_score[:, :, :], g_one[:, :, :]).then_inc(gate_step, 1)
                dve.wait_ge(gate_step, step + 2)
                other = g_score[:, :, :].unsqueeze(2).broadcast_to([P, TT, E, E])
                own = g_score[:, :, :].unsqueeze(3).broadcast_to([P, TT, E, E])
                nc.vector.tensor_tensor(g_gt[:, :, :, :], other, own, ALU.is_gt).then_inc(gate_step, 1)
                nc.vector.tensor_tensor(g_eq[:, :, :, :], other, own, ALU.is_equal).then_inc(gate_step, 1)
                dve.wait_ge(gate_step, step + 4)
                nc.vector.tensor_tensor(g_tie[:, :, :, :], g_eq[:, :, :, :],
                                        before[:, :, :].unsqueeze(1).broadcast_to([P, TT, E, E]),
                                        ALU.mult).then_inc(gate_step, 1)
                dve.wait_ge(gate_step, step + 5)
                nc.vector.tensor_tensor(g_ahead[:, :, :, :], g_gt[:, :, :, :], g_tie[:, :, :, :],
                                        ALU.add).then_inc(gate_step, 1)
                dve.wait_ge(gate_step, step + 6)
                nc.vector.reduce_sum(g_rank[:, :, :], g_ahead[:, :, :, :], AX.X).then_inc(gate_step, 1)
                dve.wait_ge(gate_step, step + 7)
                nc.vector.scalar_tensor_tensor(g_keep[:, :, :], g_rank[:, :, :], 2.0, g_score[:, :, :],
                                               ALU.is_lt, ALU.mult).then_inc(gate_step, 1)
                dve.wait_ge(gate_step, step + 8)
                nc.vector.reduce_sum(g_sum[:, :], g_keep[:, :, :], AX.X).then_inc(gate_step, 1)
                dve.wait_ge(gate_step, step + 9)
                nc.vector.reciprocal(g_rsum[:, :], g_sum[:, :]).then_inc(gate_step, 1)
                dve.wait_ge(gate_step, step + 10)
                nc.vector.tensor_tensor(g_dense[:, :, :], g_keep[:, :, :],
                                        g_rsum[:, :].unsqueeze(2).broadcast_to([P, TT, E]), ALU.mult).then_inc(gate_step, 1)
                dve.wait_ge(gate_step, step + 11)
                after(dve, denseT_in_psum, i - 1)
                nc.vector.tensor_copy(g_parts[:, :, 0, :].bitcast(f32r), g_dense[:, :, :]).then_inc(gate_step, 1)
                dve.wait_ge(gate_step, step + 12)
                nc.vector.tensor_tensor(g_parts[:, :, 1, :].bitcast(f32r), g_dense[:, :, :], g_parts[:, :, 0, :],
                                        ALU.subtract).then_inc(gate_step, 1)

            def frame(j, p):
                i = 2 * j + p
                for k in range(HALVES):
                    e = HALVES * i + k
                    if has_half(j, p, k, 1):
                        kl, par = half_buffers(p, k, 1)
                        dve.wait_ge(S_in_psum, e)
                        if kl == 0:
                            dve.wait_ge(mask_ready, i + 1)
                        after(dve, exp_done, PAIRS * (e - 2))
                        hold_waits(dve)
                        for r in range(PAIRS):
                            nc.vector.tensor_tensor_reduce(
                                out=logits[kl % 2][:, r, :], in0=S_ps[:, P * r:P * (r + 1)], in1=mask_add[par][:, kl % 4, :],
                                scale=1.0, scalar=3.0e38, op0=ALU.add, op1=ALU.min,
                                accum_out=neg_max[kl % 2][:, r:r + 1]).then_inc(logits_ready, 1)
                    if has_half(j, p, k, 2):
                        n = (k - 2) % 4
                        dve.wait_ge(exp_done, PAIRS * (e - 1))
                        after(dve, probs_ready, e - 5)
                        nc.vector.reciprocal(rdenom[n][:, :], denom[n][:, :]).then_inc(rdenom_ready, 1)
                    if k == 0 and has(j, p, 3, NG + 2):
                        dve.wait_ge(y_in_psum, i - 2)
                        after(dve, out_stored[1 - p], 16 * (j + (p - 3) // 2))
                        nc.vector.tensor_tensor(out_sb[1 - p][:, :, :], Y_ps[:, 0:GT].rearrange("p (t d) -> p t d", t=TT),
                                                x1[1 - p][:, :, :], ALU.add).then_inc(out_ready, 1)
                    tile = ffn_tile(j, p, k - 1) if k else None
                    if tile is not None:
                        r, n = tile
                        dve.wait_ge(tanh_done, n + 1)
                        after(dve, h_prod_done, n)
                        nc.vector.scalar_tensor_tensor(h_silu[:, :], h_tanh[:, :], 1.0, H_ps[:, 0:GT],
                                                       ALU.add, ALU.mult).then_inc(silu_done, 1)
                        dve.wait_ge(silu_done, n + 1)
                        if r == NT:
                            after(dve, y_in_psum, i - 2)
                            nc.vector.tensor_tensor(h[:, NT, :], h_silu[:, :], H_ps[:, 256:256 + GT],
                                                    ALU.mult).then_inc(h_prod_done, 1)
                        else:
                            after(dve, h_routed_done, NT * (i - 2) + r)
                            nc.vector.tensor_tensor(h_prod[:, :], h_silu[:, :], H_ps[:, 256:256 + GT],
                                                    ALU.mult).then_inc(h_prod_done, 1)
                            dve.wait_ge(h_prod_done, n + 1)
                            nc.vector.tensor_tensor(h[:, r, :], h_prod[:, :], Y_ps[:, 0:GT],
                                                    ALU.mult).then_inc(h_routed_done, 1)
                    if has_half(j, p, k, 3):
                        n = (k - 3) % 2
                        dve.wait_ge(pT_hi_ready, e - 2)
                        after(dve, C_in_psum, e - 4)
                        nc.vector.tensor_tensor(pT_lo[n][:, :], PT_ps[:, :], pT_hi[n][:, :].bitcast(fp32),
                                                ALU.subtract).then_inc(pT_lo_ready, 1)
                    if has_half(j, p, k, 4):
                        kl, par = half_buffers(p, k, 4)
                        dve.wait_ge(cT_hi_ready, e - 3)
                        if kl == 0:
                            after(dve, W_in_psum, i - 1)
                        hs = slice(8 * (kl // 4), 8 * (kl // 4) + 8)
                        nc.vector.tensor_tensor(cT_lo[par][:, hs, kl % 4, :], C_ps[:, :].rearrange("p (h q) -> p h q", h=8),
                                                cT_hi[par][:, hs, kl % 4, :].bitcast(fp32),
                                                ALU.subtract).then_inc(cT_lo_ready, 1)
                    if k == 7 and has(j, p, 1, NG):
                        step = 3 * (i - 1)
                        dve.wait_ge(attn_in_psum, i)
                        dve.wait_ge(x_res_loaded[1 - p], 16 * (j + (p - 1) // 2 + 1))
                        after(dve, out_ready, i - 2)
                        nc.vector.tensor_tensor(x1[1 - p][:, :, :], X_ps[:, 0:GT].rearrange("p (t d) -> p t d", t=TT),
                                                x_res[1 - p][:, :, :], ALU.add).then_inc(x1_step, 1)
                        dve.wait_ge(x1_step, step + 1)
                        for t in range(TT):
                            last = nc.vector.bn_stats(x1_bn[:, t, :], x1[1 - p][:, t, :])
                        last.then_inc(x1_step, 1)
                        dve.wait_ge(x1_step, step + 2)
                        after(dve, x2_step, X2_STEPS * (i - 1))
                        hold_waits(dve)
                        for t in range(TT):
                            last = nc.vector.bn_aggr(x1_mv[:, t, :], x1_bn[:, t, :])
                        last.then_inc(x1_step, 1)
                    if k == 1 and has(j, p, 2, NG + 1):
                        dve.wait_ge(x2T_hi_ready, i - 1)
                        after(dve, H_in_psum, HT * (i - 2))
                        nc.vector.tensor_tensor(x2T_lo[:, :], X_ps[:, 0:GT], x2T_hi[:, :].bitcast(fp32),
                                                ALU.subtract).then_inc(x2T_lo_ready, 1)
                    if k == 2 and has(j, p, -1, NG - 2):
                        dve.wait_ge(latT_hi_ready, i + 2)
                        after(dve, t_in_psum, HALVES * i)
                        nc.vector.tensor_tensor(latT_lo[1 - p][:, :, :],
                                                X_ps[:, :].rearrange("p (b f) -> p b f", b=GB)[:, :, S:P],
                                                latT_hi[1 - p][:, :, :].bitcast(fp32), ALU.subtract).then_inc(latT_lo_ready, 1)
                    if k == 3 and has(j, p, 2, NG + 1):
                        dve.wait_ge(denseT_in_psum, i - 1)
                        after(dve, H_in_psum, HT * (i - 2))
                        nc.vector.tensor_copy(denseT[:, :], X_ps[0:2 * E, 0:GT]).then_inc(denseT_ready, 1)
                    if k == 3 and has(j, p, -1, NG - 2):
                        convert_mask(j, p + 1)
                    if k == 5 and has(j, p, -2, NG - 3):
                        dve.wait_ge(kv_loaded[p], 32 * (j + 2))
                        after(dve, kv_mv_done, i + 2)
                        for b in range(GB):
                            last = nc.vector.bn_stats(kv_bn[:, b, :], kv_raw[p][:, b, :])
                        last.then_inc(kv_bn_done, 1)
                        dve.wait_ge(kv_bn_done, i + 3)
                        after(dve, kv_step, KV_STEPS * (i + 1) + 4)
                        hold_waits(dve)
                        for b in range(GB):
                            last = nc.vector.bn_aggr(kv_mv[:, b, :], kv_bn[:, b, :])
                        last.then_inc(kv_mv_done, 1)
                    if k == 2 and has(j, p, 2, NG + 1):
                        gate(i - 1)

            frames(dve, frame)

        @block.tensor
        def _(pe):
            pe.wait_ge(consts_ready, 1)
            pe.wait_ge(attn_w_loaded, 4 * 16)
            for n in range(6):
                src = (wq_raw, wk_raw, wv_raw)[n // 2]
                for c in range(4):
                    col = P * (4 * (n % 2) + c)
                    last = nc.tensor.transpose(banks[n][:, P * c:P * (c + 1)], src[:, col:col + P], ident[:, :])
                last.then_inc(wT_in_psum, 1)
            pe.wait_ge(wT_ready, 6)
            for n in range(2):
                for q in range(4):
                    for c in range(4):
                        hd = list(range(H))[bank_heads(q)][c]
                        rows = slice(DH * (hd % 2), DH * (hd % 2) + DH)
                        rhs = wT[1][rows, hd // 2, :] if n == 0 else wo_raw[rows, hd // 2, :]
                        last = nc.tensor.matmul(banks[4 * n + q][:, P * c:P * (c + 1)],
                                                wT[2 * n][rows, hd // 2, :], rhs, start=True, stop=True)
                    last.then_inc(MV_in_psum, 1)
            pe.wait_ge(MV_lo_ready, 8)
            pe.wait_ge(dve_consts, 5)
            pe.wait_ge(consts_ready, 2)

            def matmul3(dst, w_hi, w_lo, m_hi, m_lo, first=True, last=True):
                nc.tensor.matmul(dst, w_hi, m_hi, start=first, stop=False)
                nc.tensor.matmul(dst, w_hi, m_lo, start=False, stop=False)
                return nc.tensor.matmul(dst, w_lo, m_hi, start=False, stop=last)

            def frame(j, p):
                i = 2 * j + p
                for k in range(HALVES):
                    e = HALVES * i + k
                    if has_half(j, p, k, 3):
                        pe.wait_ge(probs_ready, e - 2)
                        after(pe, pT_lo_ready, e - 3)
                        for r in range(PAIRS):
                            last = nc.tensor.transpose(PT_ps[:, P * r:P * (r + 1)], probs[(k - 3) % 4][:, r, :], ident[:, :])
                        last.then_inc(pT_in_psum, 1)
                    if has_half(j, p, k, 4):
                        kl, par = half_buffers(p, k, 4)
                        pe.wait_ge(pT_lo_ready, e - 3)
                        if kl == 0:
                            pe.wait_ge(kv_step, KV_STEPS * (i + 1))
                        after(pe, cT_lo_ready, e - 4)
                        matmul3(C_ps[:, :], kv_hi[par][:, kl % 4, :], kv_lo[par][:, kl % 4, :], pT_hi[kl % 2][:, :],
                                pT_lo[kl % 2][:, :]).then_inc(C_in_psum, 1)
                    if has_half(j, p, k, 0):
                        if k == 0:
                            pe.wait_ge(kvT_ready, i + 1)
                        if k in (0, 4):
                            pe.wait_ge(t_ready, e + 4)
                        after(pe, logits_ready, PAIRS * e)
                        for r in range(PAIRS):
                            hd = 8 * (k // 4) + 2 * r
                            last = nc.tensor.matmul(S_ps[:, P * r:P * (r + 1)], tT[:, k % 4, hd:hd + 2, :],
                                                    kvT[p][:, k % 4, :], start=True, stop=True)
                        last.then_inc(S_in_psum, 1)
                    if k == 2 and has(j, p, -1, NG - 2):
                        pe.wait_ge(kv_step, KV_STEPS * (i + 1) + 6)
                        if has(j, p, 2, NG + 1):
                            pe.wait_ge(gate_exp_done, i - 1)
                        for b in range(GB):
                            last = nc.tensor.transpose(X_ps[:, P * b:P * (b + 1)], kv_f[:, b, :], ident[:, :])
                        last.then_inc(kvT_in_psum, 1)
                    chunk = query_chunk(j, p, k)
                    if chunk is not None:
                        c, ahead = chunk
                        pl = (p + ahead) % 2
                        if k == 3:
                            pe.wait_ge(latT_lo_ready, i + 2)
                        after(pe, t_ready, e + 5)
                        for n in range(2):
                            hd = 2 * c + n
                            last = matmul3(T_ps[:, GT * n:GT * (n + 1)], MV_hi[0][:, hd, :], MV_lo[0][:, hd, :],
                                           latT_hi[pl][:, :, :], latT_lo[pl][:, :, :])
                        last.then_inc(t_in_psum, 1)
                    if k == 3 and has(j, p, 2, NG + 1):
                        pe.wait_ge(gate_step, GATE_STEPS * (i - 1))
                        for t in range(TT):
                            last = nc.tensor.transpose(X_ps[0:2 * E, P * t:P * (t + 1)],
                                                       g_parts[:, t, :, :].rearrange("p a e -> p (a e)"), ident[:, :])
                        last.then_inc(denseT_in_psum, 1)
                    if k <= 5 and has(j, p, 1, NG):
                        if k == 0:
                            pe.wait_ge(cT_lo_ready, HALVES * (i - 1) + 4)
                            after(pe, attnT_ready, i - 1)
                        if k == 4:
                            pe.wait_ge(cT_lo_ready, HALVES * i)
                        for hd in range(PROJ_HEADS[k], PROJ_HEADS[k + 1]):
                            last = matmul3(W_ps[:, 0:GT], MV_hi[1][:, hd, :], MV_lo[1][:, hd, :],
                                           cT_hi[1 - p][:, hd, :, :], cT_lo[1 - p][:, hd, :, :],
                                           first=hd == 0, last=hd == H - 1)
                        if k == 5:
                            last.then_inc(W_in_psum, 1)
                    if k == 6 and has(j, p, 1, NG):
                        pe.wait_ge(attnT_ready, i)
                        if has(j, p, 2, NG + 1):
                            pe.wait_ge(denseT_ready, i - 1)
                        elif has(j, p, -1, NG - 2):
                            pe.wait_ge(latT_lo_ready, i + 2)
                        for t in range(TT):
                            last = nc.tensor.transpose(X_ps[:, P * t:P * (t + 1)], attnT[:, P * t:P * (t + 1)], ident[:, :])
                        last.then_inc(attn_in_psum, 1)
                    if k == 7 and has(j, p, 2, NG + 1):
                        pe.wait_ge(h_prod_done, HT * (i - 1))
                        pe.wait_ge(h_routed_done, NT * (i - 1))
                        for t in range(TT):
                            for n in range(HT):
                                last = nc.tensor.matmul(Y_ps[:, D * t:D * (t + 1)], h[:, n, P * t:P * (t + 1)],
                                                        w2_sb[:, n, :], start=n == 0, stop=n == HT - 1)
                        last.then_inc(y_in_psum, 1)
                    if k == 1 and has(j, p, 2, NG + 1):
                        pe.wait_ge(x2T_ready, i - 1)
                        pe.wait_ge(x2T_lo_ready, i - 1)
                        for t in range(TT):
                            last = nc.tensor.matmul(X_ps[:, E * t:E * (t + 1)], x2T[:, P * t:P * (t + 1)], gate_sb[:, :],
                                                    start=True, stop=True)
                        last.then_inc(gate_in_psum, 1)
                    tile = ffn_tile(j, p, k)
                    if tile is not None:
                        r, n = tile
                        after(pe, h_prod_done, n)
                        for a in range(2):
                            last = matmul3(H_ps[:, 256 * a:256 * a + GT], w13_hi[:, a, r, :], w13_lo[:, a, r, :],
                                           x2T_hi[:, :], x2T_lo[:, :])
                        if r != NT:
                            if r == 0:
                                pe.wait_ge(denseT_ready, i - 1)
                                after(pe, out_ready, i - 2)
                            after(pe, h_routed_done, NT * (i - 2) + r)
                            last = nc.tensor.matmul(Y_ps[:, 0:GT], expert_rows_r[:, r, :, :].rearrange("p e f -> p (e f)"),
                                                    denseT[:, :], start=True, stop=True)
                        last.then_inc(H_in_psum, 1)
                    if k == 0 and has(j, p, 2, NG + 1):
                        pe.wait_ge(x2_step, X2_STEPS * (i - 1))
                        for t in range(TT):
                            last = nc.tensor.transpose(X_ps[:, P * t:P * (t + 1)], x2[:, t, :], ident[:, :])
                        last.then_inc(x2T_in_psum, 1)

            frames(pe, frame)


_INS = ['x', 'ctx_1024', 'mask_BxS2_ik0', 'L0_xattn_ln_m_w', 'L0_xattn_ln_m_b', 'L0_xattn_ln_l_w', 'L0_xattn_ln_l_b',
        'L0_xattn_Wq', 'L0_xattn_Wk', 'L0_xattn_Wv', 'L0_xattn_Wo', 'L0_ffn_gate_w', 'L0_ffn_w1', 'L0_ffn_w3',
        'L0_ffn_w2', 'L0_ffn_ws1', 'L0_ffn_ws3', 'L0_ffn_ws2']


def kernel(**inputs):
    import numpy as _np
    import concourse.bacc as _bacc
    from concourse import mybir as _mybir
    from concourse.bass_utils import run_bass_kernel_spmd as _run

    nc = _bacc.Bacc("TRN2", target_bir_lowering=False, num_devices=1)
    arrays, args = {}, []
    for name in _INS:
        a = _np.ascontiguousarray(inputs[name])
        arrays[f"in_{name}"] = a
        args.append(nc.dram_tensor(f"in_{name}", a.shape, _mybir.dt.from_np(a.dtype), kind="ExternalInput").ap())
    out = nc.dram_tensor("out_0", arrays["in_x"].shape, _mybir.dt.float32, kind="ExternalOutput").ap()
    xattn_moe_ffn_kernel(nc, *args, out)
    r = _run(nc, [arrays], core_ids=[0])
    return r.results[0]["out_0"]
```
